# Optimizing a Trainium2 kernel written in Bass

```python
import numpy as np
import jax
import jax.numpy as jnp

def _softmax(x, axis=-1):
    return jax.nn.softmax(x, axis=axis)

def _gelu(x):
    return jax.nn.gelu(x, approximate=True)

def _silu(x):
    return jax.nn.silu(x)

def _sigmoid(x):
    return jax.nn.sigmoid(x)

def _layernorm(x, axis=-1, eps=1e-05):
    m = jnp.mean(x, axis=axis, keepdims=True)
    v = jnp.var(x, axis=axis, keepdims=True)
    return (x - m) / jnp.sqrt(v + eps)

def _scatter_add(tgt, idx, src, axis=0):
    return tgt.at[idx].add(src)

def _segment_sum(src, seg, n):
    return jax.ops.segment_sum(src, seg, n)
kernel_name = 'mk_audio_tower_d1_tok_audfeat256_r4_e8a9aa'

def setup_inputs(seed: int=0):
    np.random.seed(seed)
    _w = jnp.asarray

    def _rec_inputs():
        import jax
        import jax.numpy as jnp
        _rk = jax.random.key(seed)
        x = -0.000392918 + 0.999932 * jax.random.normal(jax.random.fold_in(_rk, 1), (4, 750, 64), jnp.float32)
        return x
    x = _rec_inputs()

    def _L0_tok_setup():
        import jax, jax.numpy as jnp
        import numpy as np
        from jax import lax
        B, S, CIN, COUT, K = (32, 512, 64, 64, 16)
        key = jax.random.key(seed)
        k1, k2, k3, k4 = jax.random.split(key, 4)
        x = jax.random.normal(k1, (B, S, CIN), dtype=jnp.float32)
        w_real = jax.random.normal(k2, (COUT, CIN, K), dtype=jnp.float32) * 0.1
        w_imag = jax.random.normal(k3, (COUT, CIN, K), dtype=jnp.float32) * 0.1
        phases = jax.random.normal(k4, (K,), dtype=jnp.float32) * 0.1
        return {'x': x, 'w_real': w_real, 'w_imag': w_imag, 'phases': phases}
    _L0_tok_all = _L0_tok_setup()
    _L0_tok_in = {k: v for k, v in _L0_tok_all.items() if k in ('w_real', 'w_imag', 'phases')}
    del _L0_tok_all

    def _L0_attn_setup():
        import jax, jax.numpy as jnp
        import numpy as np
        EMBED_DIM = 64
        SEQ_LEN = 1024
        BATCH = 8
        ALPHA = 0.99
        key = jax.random.key(seed)
        k_x, k_w, k_b = jax.random.split(key, 3)
        x = jax.random.normal(k_x, (BATCH, SEQ_LEN, EMBED_DIM), dtype=jnp.float32)
        Wqkv = jax.random.normal(k_w, (EMBED_DIM, 3 * EMBED_DIM), dtype=jnp.float32) * EMBED_DIM ** (-0.5)
        bqkv = jax.random.normal(k_b, (3 * EMBED_DIM,), dtype=jnp.float32) * 0.02
        return {'x': x, 'Wqkv': Wqkv, 'bqkv': bqkv}
    _L0_attn_all = _L0_attn_setup()
    _L0_attn_in = {k: v for k, v in _L0_attn_all.items() if k in ('Wqkv', 'bqkv')}
    del _L0_attn_all

    def _L0_ffn_setup():
        import jax, jax.numpy as jnp
        import numpy as np
        B, T, C = (64, 96, 64)
        NH, NKV = (4, 2)
        HD = C // NH
        NREP = NH // NKV
        NE, TOPK = (8, 2)
        HID = int(8 / 3 * C)
        EPS_RMS = 1e-06

        def _rope_tables(t_len):
            inv_freq = 1.0 / 10000.0 ** (np.arange(0, HD, 2, dtype=np.float32) / HD)
            t = np.arange(t_len, dtype=np.float32)
            freqs = np.outer(t, inv_freq)
            emb = np.concatenate([freqs, freqs], axis=-1)
            return (jnp.asarray(np.cos(emb)), jnp.asarray(np.sin(emb)))

        def _rotate_half(x):
            h = x.shape[-1] // 2
            return jnp.concatenate([-x[..., h:], x[..., :h]], axis=-1)

        def _rmsnorm(v, w):
            return v * jax.lax.rsqrt(jnp.mean(v * v, axis=-1, keepdims=True) + EPS_RMS) * w
        key = jax.random.key(seed)
        ks = jax.random.split(key, 10)
        s = lambda k, shape: jax.random.normal(k, shape, jnp.float32) * 0.02
        return {'x': jax.random.normal(ks[0], (B, T, C), jnp.float32), 'ln1_w': jnp.ones((C,), jnp.float32), 'ln2_w': jnp.ones((C,), jnp.float32), 'wq': s(ks[1], (NH * HD, C)), 'wk': s(ks[2], (NKV * HD, C)), 'wv': s(ks[3], (NKV * HD, C)), 'wo': s(ks[4], (C, C)), 'router_w': s(ks[5], (NE, C)), 'w1': s(ks[6], (NE, HID, C)), 'w2': s(ks[7], (NE, C, HID)), 'w3': s(ks[8], (NE, HID, C))}
    _L0_ffn_all = _L0_ffn_setup()
    _L0_ffn_in = {k: v for k, v in _L0_ffn_all.items() if k in ('ln1_w', 'ln2_w', 'wq', 'wk', 'wv', 'wo', 'router_w', 'w1', 'w2', 'w3')}
    del _L0_ffn_all
    return {'x': x, 'L0_tok_w_real': _L0_tok_in['w_real'], 'L0_tok_w_imag': _L0_tok_in['w_imag'], 'L0_tok_phases': _L0_tok_in['phases'], 'L0_attn_Wqkv': _L0_attn_in['Wqkv'], 'L0_attn_bqkv': _L0_attn_in['bqkv'], 'L0_ffn_ln1_w': _L0_ffn_in['ln1_w'], 'L0_ffn_ln2_w': _L0_ffn_in['ln2_w'], 'L0_ffn_wq': _L0_ffn_in['wq'], 'L0_ffn_wk': _L0_ffn_in['wk'], 'L0_ffn_wv': _L0_ffn_in['wv'], 'L0_ffn_wo': _L0_ffn_in['wo'], 'L0_ffn_router_w': _L0_ffn_in['router_w'], 'L0_ffn_w1': _L0_ffn_in['w1'], 'L0_ffn_w2': _L0_ffn_in['w2'], 'L0_ffn_w3': _L0_ffn_in['w3']}

def reference(x, L0_tok_w_real, L0_tok_w_imag, L0_tok_phases, L0_attn_Wqkv, L0_attn_bqkv, L0_ffn_ln1_w, L0_ffn_ln2_w, L0_ffn_wq, L0_ffn_wk, L0_ffn_wv, L0_ffn_wo, L0_ffn_router_w, L0_ffn_w1, L0_ffn_w2, L0_ffn_w3):
    import jax
    import jax.numpy as jnp

    def _L0_tok_ref(x, w_real, w_imag, phases):
        import jax, jax.numpy as jnp
        import numpy as np
        from jax import lax
        B, S, CIN, COUT, K = (32, 512, 64, 64, 16)
        w_eff = jnp.cos(phases)[None, None, :] * w_real - jnp.sin(phases)[None, None, :] * w_imag
        y = lax.conv_general_dilated(jnp.transpose(x, (0, 2, 1)), w_eff, window_strides=(1,), padding='VALID', dimension_numbers=('NCH', 'OIH', 'NCH'))
        return jnp.transpose(y, (0, 2, 1))

    def _L0_attn_ref(x, Wqkv, bqkv):
        import jax, jax.numpy as jnp
        import numpy as np
        EMBED_DIM = 64
        SEQ_LEN = 1024
        BATCH = 8
        ALPHA = 0.99
        bs, sl, d = x.shape
        qkv = x @ Wqkv + bqkv
        q, k, v = jnp.split(qkv, 3, axis=-1)
        i = jnp.arange(sl, dtype=jnp.float32)
        M = jnp.where(i[:, None] >= i[None, :], jnp.power(jnp.float32(ALPHA), i[:, None] - i[None, :]), 0.0)
        scores = jnp.einsum('bqd,bkd->bqk', q, k) / jnp.sqrt(jnp.float32(d))
        out = jnp.einsum('bqk,bkd->bqd', scores * M, v)
        return out

    def _L0_ffn_ref(x, ln1_w, ln2_w, wq, wk, wv, wo, router_w, w1, w2, w3):
        import jax, jax.numpy as jnp
        import numpy as np
        B, T, C = (64, 96, 64)
        NH, NKV = (4, 2)
        HD = C // NH
        NREP = NH // NKV
        NE, TOPK = (8, 2)
        HID = int(8 / 3 * C)
        EPS_RMS = 1e-06

        def _rope_tables(t_len):
            inv_freq = 1.0 / 10000.0 ** (np.arange(0, HD, 2, dtype=np.float32) / HD)
            t = np.arange(t_len, dtype=np.float32)
            freqs = np.outer(t, inv_freq)
            emb = np.concatenate([freqs, freqs], axis=-1)
            return (jnp.asarray(np.cos(emb)), jnp.asarray(np.sin(emb)))

        def _rotate_half(x):
            h = x.shape[-1] // 2
            return jnp.concatenate([-x[..., h:], x[..., :h]], axis=-1)

        def _rmsnorm(v, w):
            return v * jax.lax.rsqrt(jnp.mean(v * v, axis=-1, keepdims=True) + EPS_RMS) * w
        Bx, Tx, Cx = x.shape
        h = _rmsnorm(x, ln1_w)
        q = (h @ wq.T).reshape(Bx, Tx, NH, HD).transpose(0, 2, 1, 3)
        k = (h @ wk.T).reshape(Bx, Tx, NKV, HD).transpose(0, 2, 1, 3)
        v = (h @ wv.T).reshape(Bx, Tx, NKV, HD).transpose(0, 2, 1, 3)
        cos, sin = _rope_tables(Tx)
        cos, sin = (cos[None, None], sin[None, None])
        q = q * cos + _rotate_half(q) * sin
        k = k * cos + _rotate_half(k) * sin
        k = jnp.repeat(k, NREP, axis=1)
        v = jnp.repeat(v, NREP, axis=1)
        scores = jnp.einsum('bhtd,bhsd->bhts', q, k) / jnp.sqrt(jnp.float32(HD))
        causal = jnp.tril(jnp.ones((Tx, Tx), dtype=bool))
        scores = jnp.where(causal[None, None], scores, jnp.float32(-1e+30))
        att = jax.nn.softmax(scores, axis=-1)
        y = jnp.einsum('bhts,bhsd->bhtd', att, v).transpose(0, 2, 1, 3).reshape(Bx, Tx, Cx)
        x = x + y @ wo.T
        flat = _rmsnorm(x, ln2_w).reshape(-1, Cx)
        probs = jax.nn.softmax(flat @ router_w.T, axis=-1)
        tp, ti = jax.lax.top_k(probs, TOPK)
        tp = tp / (jnp.sum(tp, axis=-1, keepdims=True) + 1e-09)
        weights = jnp.sum(tp[..., None] * jax.nn.one_hot(ti, NE, dtype=flat.dtype), axis=1)
        out = jnp.zeros_like(flat)
        for e in range(NE):
            hh = jax.nn.silu(flat @ w1[e].T) * (flat @ w3[e].T)
            out = out + weights[:, e:e + 1] * (hh @ w2[e].T)
        return x + out.reshape(Bx, Tx, Cx)
    h = _L0_tok_ref(x, L0_tok_w_real, L0_tok_w_imag, L0_tok_phases)
    h = h + _L0_attn_ref(_layernorm(h, axis=-1), L0_attn_Wqkv, L0_attn_bqkv)
    h = h + _L0_ffn_ref(_layernorm(h, axis=-1), L0_ffn_ln1_w, L0_ffn_ln2_w, L0_ffn_wq, L0_ffn_wk, L0_ffn_wv, L0_ffn_wo, L0_ffn_router_w, L0_ffn_w1, L0_ffn_w2, L0_ffn_w3)
    return h

_drawn_inputs = setup_inputs


def setup_inputs(seed=0):
    import zlib

    import numpy as np

    out = dict(_drawn_inputs(seed))
    spreads = {'L0_ffn_ln1_w': (1.0, 0.6), 'L0_ffn_ln2_w': (1.0, 0.6)}
    factors = {'L0_ffn_wq': 8.0,
     'L0_ffn_wk': 8.0,
     'L0_ffn_wv': 8.0,
     'L0_ffn_wo': 8.0,
     'L0_ffn_router_w': 8.0,
     'L0_ffn_w1': 8.0,
     'L0_ffn_w2': 8.0,
     'L0_ffn_w3': 8.0}
    for name, (base, spread) in spreads.items():
        noise = np.random.default_rng([zlib.crc32(name.encode()), seed]).standard_normal(out[name].shape)
        drawn = base * np.exp(spread * noise) if base else spread * noise
        out[name] = jnp.asarray(drawn.astype(out[name].dtype))
    for name, factor in factors.items():
        out[name] = (out[name] * factor).astype(out[name].dtype)
    return out
```

```python
from contextlib import ExitStack

import numpy as np

import concourse.bass as bass
from concourse import mybir

B, S_IN, C, TAPS = 4, 750, 64, 16
TV = S_IN - TAPS + 1
T = TV + TV % 2
TP = 768
HALF = T // 2
PAIRS = B // 2
NB = (T + 127) // 128
WIDTH = [T - 128 * j for j in range(NB)]
ROWS = [min(128, w) for w in WIDTH]
NH, NKV, HD = 4, 2, 16
NE, HID = 8, int(8 / 3 * C)
NM = (NE * HID + 127) // 128
MP = NM * 128
XW = S_IN + 2
ALPHA = float(np.float32(0.99))
NEG = -1e30
RING = 3
TRIG_STEPS = 7
ROUND = 12582912.0
PT = 6
DVE_STEPS = 24


def pieces(width):
    return [(0, width)] if width <= 512 else [(0, width // 2), (width // 2, width // 2)]


def score_rounds():
    out = []
    for i in range(NB):
        w = min(128 * (i + 1), T)
        n = {128: 4, 256: 4, 384: 2, 512: 2}.get(w, 1)
        out += [(i, w, tuple(range(h, h + n))) for h in range(0, NH, n)]
    return out


def slot_plan():
    order = ["conv", "cen1", "var1", "linq", "link", "linv"]
    order += [("lin", j, b) for j in range(NB) for b in range(2)]
    order += ["cen2", "var2", "ms1", "q", "qperm", "k", "v"]
    for b in range(2):
        order += [("max", b, n) for n in range(len(score_rounds()))]
        order += [("negmax", b)]
    for b in range(2):
        order += [("score", b, j, h) for j in range(NB) for h in range(NH)]
        order += [("den", b), ("wo", b)]
    order += ["ms2", "router", "rwT"]
    order += [("moe", c, m, b) for c in range(2) for m in range(NM) for b in range(2)]
    order += ["outT"]
    used, plan = [0] * RING, {}
    for n, step in enumerate(order):
        plan[step] = (n % RING, used[n % RING])
        used[n % RING] += 1
    return plan, used


def audio_tower(nc, xT, wr, wi, ph, lin_w, lin_bqk, lin_bv, ln_w, qkv_w, wo_w, router_w,
                w1T, w3T, w2T, eye, cen, avg, dsel,
                qdec, kdec, qcos, qsin, ktab, rank, mask01, out):
    f32, f32r, bf16 = mybir.dt.float32, mybir.dt.float32r, mybir.dt.bfloat16
    ALU, ACT, AX = mybir.AluOpType, mybir.ActivationFunctionType, mybir.AxisListType

    q_scr = nc.dram_tensor("q_scratch", [2, 2, NH, HD, T], f32).ap()
    k_scr = nc.dram_tensor("k_scratch", [2, 2, NKV, HD, T], f32).ap()
    w_scr = nc.dram_tensor("route_scratch", [2, NE, T], f32).ap()

    with ExitStack() as ctx:
        def sb(name, shape, dt=f32):
            return ctx.enter_context(nc.sbuf_tensor(name, shape, dt))

        w_conv = sb("w_conv", [128, 8, C])
        phase = sb("phase", [128, 8])
        trig = sb("trig", [128, 2, 8])
        turns = sb("turns", [128, 2, 8])
        lin_ws = sb("lin_ws", [128, 3, 128])
        lin_b = sb("lin_b", [128, 2])
        lin_vb = sb("lin_vb", [128, 128])
        ln_ws = sb("ln_ws", [128, 2])
        qkv_ws = sb("qkv_ws", [128, 3 * 128 + 64])
        wo_ws = sb("wo_ws", [128, C])
        router_ws = sb("router_ws", [128, 2 * NE])
        w_hi = [sb(f"w{n}_hi", [128, MP], f32r) for n in (1, 3)]
        w_lo = [sb(f"w{n}_lo", [128, MP], f32r) for n in (1, 3)]
        w2_ws = sb("w2_ws", [128, NM, C])
        ident = sb("ident", [128, 128])
        center = sb("center", [128, 128])
        average = sb("average", [128, 128])
        den_sel = sb("den_sel", [128, 128])
        q_decay = sb("q_decay", [128, T])
        k_decay = sb("k_decay", [128, T])
        q_cos = sb("q_cos", [128, T])
        q_sin = sb("q_sin", [128, T])
        k_tab = sb("k_tab", [128, T])
        rank_t = sb("rank_t", [128, NE])
        keep01 = sb("keep01", [128, 128])
        eye_b = sb("eye_b", [128, 128], bf16)
        neg_qk = sb("neg_qk", [128, 128], bf16)
        neg_kq = sb("neg_kq", [128, 128], bf16)
        eps = sb("eps", [128, 2])
        spare = sb("spare", [128, 6])

        x_in = sb("x_in", [128, 2, XW])
        h = sb("h", [128, TP])
        cent = sb("cent", [128, TP])
        sq = sb("sq", [128, TP])
        rs = sb("rs", [128, TP])
        xn = sb("xn", [128, TP])
        tmp1 = sb("tmp1", [128, TP])
        tmp2 = sb("tmp2", [128, TP])
        kz = [sb(f"kz{b}", [128, TP]) for b in range(2)]
        v_lin = sb("v_lin", [128, NB, 128])
        p_lin = [sb(f"p_lin{n}", [128, T]) for n in range(2)]
        h2 = sb("h2", [128, TP])
        x2 = sb("x2", [128, TP])
        parts = [sb(f"part{n}", [128, T], f32r) for n in range(2)]
        kparts = [sb(f"kpart{n}", [64, T], f32r) for n in range(2)]
        qs = [sb(f"qs{b}", [128, NH, T], f32r) for b in range(2)]
        ks = [sb(f"ks{b}", [128, NKV, T], f32r) for b in range(2)]
        v_aug = [sb(f"v_aug{b}", [128, NB, NKV, 32]) for b in range(2)]
        smax = sb("smax", [128, NB, NH])
        nmx = sb("nmx", [128, NB, NH, 2])
        nmh = sb("nmh", [128, NB, NH], f32r)
        pt = [sb(f"pt{n}", [128, T]) for n in range(PT)]
        wb = sb("wb", [128, NM, 2, HALF])
        lg, ta, tb, oh = (sb(n, [128, 2 * NB, NE]) for n in ("lg", "ta", "tb", "oh"))
        s1, s2, s3 = (sb(n, [128, 2 * NB]) for n in ("s1", "s2", "s3"))
        w_real, w_imag = (pt[n][:, 0:8 * C].rearrange("p (j c) -> p j c", c=C) for n in (2, 3))
        flat, rot, fin, xs = tmp1, sq, h, parts
        nrow, r_wT = tmp2[0:2 * NH, :], tmp2[0:2 * NE, :]
        gate = [p_lin[n // 2][:, n % 2 * HALF:(n % 2 + 1) * HALF] for n in range(4)]
        hid = [pt[n // 2][:, n % 2 * HALF:(n % 2 + 1) * HALF] for n in range(4)]
        o_t = v_lin[:].rearrange("p i (b c) -> p i b c", b=2)

        work = [ctx.enter_context(nc.psum_tensor(f"work{n}", [128, 2, 512], f32)) for n in range(RING)]
        acc = ctx.enter_context(nc.psum_tensor("acc", [128, 2, 512], f32))

        plan, uses = slot_plan()

        class Signal:

            def __init__(self, name, per_pair, start=0):
                self.sem = ctx.enter_context(nc.semaphore(name))
                self.per, self.start = per_pair, start

            def at(self, p, n):
                return p * self.per + (n + self.start)

        def once(name):
            return ctx.enter_context(nc.semaphore(name))

        full = [Signal(f"slot_full{n}", uses[n]) for n in range(RING)]
        free = [Signal(f"slot_free{n}", uses[n], start=1) for n in range(RING)]
        acc_free = Signal("acc_free", 4, start=1)
        x_loaded = Signal("x_loaded", 64)
        stored = Signal("stored", 64)
        dve_step = Signal("dve_step", DVE_STEPS)
        sq_ready = Signal("sq_ready", 4)
        rs_ready = Signal("rs_ready", 4)
        xn_ready = Signal("xn_ready", 2)
        pl_masked = Signal("pl_masked", 2 * NB)
        pl_used = [Signal(f"pl_used{n}", NB, start=1) for n in range(2)]
        kz_ready = Signal("kz_ready", 1)
        vl_ready = Signal("vl_ready", 1)
        x2_ready = Signal("x2_ready", 1)
        q_parts = Signal("q_parts", 2)
        k_parts = Signal("k_parts", 2)
        qk_out = Signal("qk_out", 64)
        stacks = [Signal(f"stack{b}", 16 * 9) for b in range(2)]
        v_ready = Signal("v_ready", 1)
        nm_ready = Signal("nm_ready", 4)
        m_in = Signal("m_in", 2 * 16 * NH)
        p_used = Signal("p_used", 2 * NB, start=2)
        rd_ready = Signal("rd_ready", 2)
        yn_ready = Signal("yn_ready", 2)
        base_ready = Signal("base_ready", 1)
        flat_ready = Signal("flat_ready", 1)
        xhi_ready = Signal("xhi_ready", 2)
        xlo_ready = Signal("xlo_ready", 2)
        lge_ready = Signal("lge_ready", 1)
        rw_ready = Signal("rw_ready", 1)
        rw_out = Signal("rw_out", 16)
        segments = [[] for _ in range(NM)]
        for e in range(NE):
            at = e * HID
            while at < (e + 1) * HID:
                end = min((e + 1) * HID, (at // 128 + 1) * 128)
                segments[at // 128].append((at % 128, at % 128 + end - at, e))
                at = end
        wb_in = [Signal(f"wb_in{m}", 4 * 16 * len(segments[m])) for m in range(NM)]
        NG = 4 * NM
        gate_ready = Signal("gate_ready", NG)
        hid_ready = Signal("hid_ready", NG)
        hid_used = Signal("hid_used", 2 * NM, start=2)
        fin_ready = Signal("fin_ready", 1)
        small_in, big_in, conv_in = once("small_in"), once("big_in"), once("conv_in")
        pool_made, dve_made = once("pool_made"), once("dve_made")
        wsplit, trig_step, sines, conv_w = once("wsplit"), once("trig_step"), once("sines"), once("conv_w")

        block = ctx.enter_context(nc.Block())

        small = [(lin_ws[:], lin_w), (lin_b[:], lin_bqk), (lin_vb[:], lin_bv), (ln_ws[:], ln_w),
                 (qkv_ws[:], qkv_w), (wo_ws[:], wo_w), (router_ws[:], router_w), (ident[:], eye),
                 (center[:], cen), (average[:], avg), (den_sel[:], dsel), (rank_t[:], rank),
                 (keep01[:], mask01), (q_decay[:], qdec), (k_decay[:], kdec),
                 (q_cos[:], qcos), (q_sin[:], qsin), (k_tab[:], ktab)]
        SMALL = 16 * len(small)
        raw = [wb[:, 2 * n:2 * n + 2].rearrange("p a b t -> p (a b t)")[:, 0:MP] for n in range(2)]
        BIG = 48
        POOL_MADE, DVE_MADE = 16, 9

        def slot(step):
            return work[plan[step][0]]

        def wait_free(eng, p, step):
            n, k = plan[step]
            eng.wait_ge(free[n].sem, free[n].at(p, k))

        def wait_full(eng, p, step):
            n, k = plan[step]
            eng.wait_ge(full[n].sem, full[n].at(p, k + 1))

        def wait_read(eng, p, step):
            n, k = plan[step]
            eng.wait_ge(free[n].sem, free[n].at(p, k + 1))

        def halves(tile):
            return tile[:, 0:T].rearrange("p (a t) -> p a t", a=2)


        @block.sync
        def _(sp):
            sp.dma_start(phase[:], ph).then_inc(conv_in, 16)
            sp.dma_start(pt[2][:, 0:8 * C], wr).then_inc(conv_in, 16)
            sp.dma_start(pt[3][:, 0:8 * C], wi).then_inc(conv_in, 16)
            for tile, src in small:
                sp.dma_start(tile, src).then_inc(small_in, 16)
            sp.dma_start(raw[0], w1T).then_inc(big_in, 16)
            sp.dma_start(raw[1], w3T).then_inc(big_in, 16)
            sp.dma_start(w2_ws[:].rearrange("p m c -> p (m c)"), w2T).then_inc(big_in, 16)
            sp.wait_ge(pool_made, POOL_MADE)
            sp.wait_ge(wsplit, 4)
            with sp.Fori(0, PAIRS) as p:
                for n in range(2):
                    sp.wait_ge(q_parts.sem, q_parts.at(p, n + 1))
                    sp.dma_start(q_scr[n].rearrange("b h d t -> (b h d) t"), parts[n][:].bitcast(f32)).then_inc(qk_out.sem, 16)
                for n in range(2):
                    sp.wait_ge(k_parts.sem, k_parts.at(p, n + 1))
                    sp.dma_start(k_scr[n].rearrange("b h d t -> (b h d) t"), kparts[n][:].bitcast(f32)).then_inc(qk_out.sem, 16)
                sp.wait_ge(qk_out.sem, qk_out.at(p, 64))
                for b in range(2):
                    for r in range(4):
                        rows = slice(16 * r, 16 * r + 16)
                        sp.dma_start(ks[b][rows].bitcast(f32), k_scr[r % 2, b].rearrange("h d t -> d h t"))\
                          .then_inc(stacks[b].sem, 16)
                        sp.dma_start(qs[b][rows].bitcast(f32), q_scr[r // 2, b].rearrange("h d t -> d h t"))\
                          .then_inc(stacks[b].sem, 16)
                    sp.dma_start(qs[b][64:66].bitcast(f32), kz[0][64:66, 0:T].unsqueeze(1).broadcast_to([2, NH, T])).then_inc(stacks[b].sem, 16)
                for b in range(2):
                    wait_read(sp, p, ("negmax", b))
                    for hh in range(NH):
                        sp.dma_start(qs[b][64:66, hh, :].bitcast(f32), nrow[2 * hh:2 * hh + 2, 0:T])\
                          .then_inc(m_in.sem, 16)
                wait_read(sp, p, "rwT")
                sp.dma_start(w_scr.rearrange("b e t -> (b e) t"), r_wT[:, 0:T]).then_inc(rw_out.sem, 16)
                sp.wait_ge(rw_out.sem, rw_out.at(p, 16))
                for c in range(2):
                    for m in range(NM):
                        if c:
                            sp.wait_ge(hid_ready.sem, hid_ready.at(p, 2 * m + 2))
                        for r0, r1, e in segments[m]:
                            for b in range(2):
                                sp.dma_start(wb[r0:r1, m, b, :],
                                             w_scr[b, e:e + 1, c * HALF:(c + 1) * HALF].broadcast_to([r1 - r0, HALF]))\
                                  .then_inc(wb_in[m].sem, 16)

        @block.gpsimd
        def _(pool):
            for tile in (eye_b, neg_qk, neg_kq):
                nc.gpsimd.memset(tile[:], 0.0).then_inc(pool_made, 1)
            for b in range(2):
                nc.gpsimd.memset(v_aug[b][:], 0.0).then_inc(pool_made, 1)
                nc.gpsimd.memset(qs[b][:].bitcast(f32), 0.0).then_inc(pool_made, 1)
                nc.gpsimd.memset(ks[b][:].bitcast(f32), 0.0).then_inc(pool_made, 1)
            pool.wait_ge(pool_made, 9)
            nc.gpsimd.affine_select(out=eye_b[:], in_=eye_b[:], compare_op=ALU.not_equal, fill=1.0, base=0,
                                    pattern=[[-1, 128]], channel_multiplier=1).then_inc(pool_made, 1)
            nc.gpsimd.affine_select(out=neg_qk[:], in_=neg_qk[:], compare_op=ALU.is_ge, fill=NEG, base=0,
                                    pattern=[[-1, 128]], channel_multiplier=1).then_inc(pool_made, 1)
            nc.gpsimd.affine_select(out=neg_kq[:], in_=neg_kq[:], compare_op=ALU.is_ge, fill=NEG, base=0,
                                    pattern=[[1, 128]], channel_multiplier=-1).then_inc(pool_made, 1)
            for b in range(2):
                pool.wait_ge(pool_made, 12 + 2 * b)
                nc.gpsimd.memset(ks[b][64:66].bitcast(f32), 1.0).then_inc(pool_made, 1)
                pool.wait_ge(pool_made, 13 + 2 * b)
                nc.gpsimd.memset(v_aug[b][:, :, :, HD:HD + 1], 1.0).then_inc(pool_made, 1)
            with pool.Fori(0, PAIRS) as p:
                for j in range(NB):
                    for b in range(2):
                        wait_read(pool, p, ("lin", j, b))
                        part = p_lin[b][0:ROWS[j], 0:ROWS[j]]
                        nc.gpsimd.tensor_tensor(part, part, keep01[0:ROWS[j], 0:ROWS[j]], ALU.mult)\
                          .then_inc(pl_masked.sem, 1)
                for b in range(2):
                    wait_read(pool, p, ("wo", b))
                nc.gpsimd.tensor_tensor(h2[:, 0:T], h2[:, 0:T], x2[:, 0:T], ALU.add).then_inc(base_ready.sem, 1)

        @block.scalar
        def _(act):
            act.wait_ge(trig_step, TRIG_STEPS)
            nc.scalar.activation(trig[:], trig[:], ACT.Sin).then_inc(sines, 1)
            act.wait_ge(dve_made, DVE_MADE)
            act.wait_ge(pool_made, POOL_MADE)

            def inverse_root(p, step, which):
                wait_full(act, p, step)
                n, _ = plan[step]
                nc.scalar.activation(halves(rs), slot(step)[:, :, 0:HALF], ACT.Ln,
                                     bias=eps[:, which:which + 1]).then_inc(free[n].sem, 1)
                wait_read(act, p, step)
                nc.scalar.activation(rs[:, 0:T], rs[:, 0:T], ACT.Exp, scale=-0.5).then_inc(rs_ready.sem, 1)

            with act.Fori(0, PAIRS) as p:
                for b in range(2):
                    for r in range(2):
                        act.dma_start(x_in[64 * r:64 * r + 64, b, 0:XW - 1], xT[p, b, :, r:r + XW - 1])\
                           .then_inc(x_loaded.sem, 16)
                wait_full(act, p, "conv")
                nc.scalar.activation(halves(h), slot("conv")[:, :, 0:HALF], ACT.Copy)\
                  .then_inc(free[plan["conv"][0]].sem, 1)
                wait_read(act, p, "cen1")
                nc.scalar.activation(sq[:, 0:T], cent[:, 0:T], ACT.Square).then_inc(sq_ready.sem, 1)
                inverse_root(p, "var1", 0)
                for j in range(NB):
                    for b in range(2):
                        step = ("lin", j, b)
                        wait_full(act, p, step)
                        act.wait_ge(pl_used[b].sem, pl_used[b].at(p, j))
                        cut = pieces(WIDTH[j])
                        w = cut[0][1]
                        nc.scalar.activation(
                            p_lin[b][0:ROWS[j], 0:WIDTH[j]].rearrange("p (a t) -> p a t", t=w),
                            slot(step)[0:ROWS[j], 0:len(cut), 0:w], ACT.Copy).then_inc(free[plan[step][0]].sem, 1)
                wait_read(act, p, "cen2")
                nc.scalar.activation(sq[:, 0:T], cent[:, 0:T], ACT.Square).then_inc(sq_ready.sem, 1)
                inverse_root(p, "var2", 0)
                act.wait_ge(x2_ready.sem, x2_ready.at(p, 1))
                nc.scalar.activation(sq[:, 0:T], x2[:, 0:T], ACT.Square).then_inc(sq_ready.sem, 1)
                inverse_root(p, "ms1", 1)
                wait_full(act, p, "v")
                vals = slot("v")[:, 0, 0:NB * 64].rearrange("p (i b h d) -> p i b h d", i=NB, b=2, h=NKV)
                nc.scalar.activation(v_aug[0][:, :, :, 0:HD], vals[:, :, 0], ACT.Copy).then_inc(v_ready.sem, 1)
                nc.scalar.activation(v_aug[1][:, :, :, 0:HD], vals[:, :, 1], ACT.Copy)\
                  .then_inc(free[plan["v"][0]].sem, 1)
                for b in range(2):
                    step = ("negmax", b)
                    wait_full(act, p, step)
                    if b:
                        act.wait_ge(m_in.sem, m_in.at(p, 64))
                    nc.scalar.activation(nrow.rearrange("p (a t) -> p a t", a=2),
                                         slot(step)[0:2 * NH, :, 0:384], ACT.Copy).then_inc(free[plan[step][0]].sem, 1)
                for b in range(2):
                    for j in range(NB):
                        for hh in range(NH):
                            step, n = ("score", b, j, hh), NH * j + hh
                            wait_full(act, p, step)
                            act.wait_ge(p_used.sem, p_used.at(p, (NH * NB * b + n - PT) // NH + 1))
                            cut = pieces(WIDTH[j])
                            w = cut[0][1]
                            nc.scalar.activation(
                                pt[n % PT][0:ROWS[j], 0:WIDTH[j]].rearrange("p (a t) -> p a t", t=w),
                                slot(step)[0:ROWS[j], 0:len(cut), 0:w], ACT.Exp).then_inc(free[plan[step][0]].sem, 1)
                    act.wait_ge(p_used.sem, p_used.at(p, NB * (b + 1)))
                    if b:
                        act.wait_ge(yn_ready.sem, yn_ready.at(p, 1))
                    nc.scalar.activation(halves(cent), acc[:, :, 0:HALF], ACT.Copy).then_inc(acc_free.sem, 1)
                    step = ("den", b)
                    wait_full(act, p, step)
                    nc.scalar.activation(halves(rs), slot(step)[:, :, 0:HALF], ACT.Ln)\
                      .then_inc(free[plan[step][0]].sem, 1)
                    wait_read(act, p, step)
                    nc.scalar.activation(rs[:, 0:T], rs[:, 0:T], ACT.Exp, scale=-1.0).then_inc(rd_ready.sem, 1)
                for b in range(2):
                    wait_read(act, p, ("wo", b))
                nc.scalar.activation(sq[:, 0:T], x2[:, 0:T], ACT.Square).then_inc(sq_ready.sem, 1)
                inverse_root(p, "ms2", 1)
                act.wait_ge(flat_ready.sem, flat_ready.at(p, 1))
                for b in range(2):
                    rows = slice(64 * b, 64 * b + 64)
                    nc.scalar.activation(xs[b][rows], flat[rows, 0:T], ACT.Copy).then_inc(xhi_ready.sem, 1)
                wait_read(act, p, "router")
                nc.scalar.activation(ta[:], lg[:], ACT.Exp).then_inc(lge_ready.sem, 1)
                wait_full(act, p, "rwT")
                nc.scalar.activation(r_wT.rearrange("p (a t) -> p a t", a=2), slot("rwT")[0:2 * NE, :, 0:384],
                                     ACT.Copy).then_inc(free[plan["rwT"][0]].sem, 1)
                for c in range(2):
                    for m in range(NM):
                        for b in range(2):
                            step, n = ("moe", c, m, b), (c * NM + m) * 2 + b
                            wait_full(act, p, step)
                            if n >= 4:
                                wait_read(act, p, ("moe", (n - 4) // (2 * NM), (n - 4) // 2 % NM, b))
                            nc.scalar.activation(gate[n % 4], slot(step)[:, 0, 0:HALF], ACT.Silu)\
                              .then_inc(gate_ready.sem, 1)
                wait_full(act, p, "outT")
                nc.scalar.activation(v_lin[:].rearrange("p (a i) c -> p a (i c)", a=2),
                                     slot("outT")[:, :, 0:384], ACT.Copy).then_inc(free[plan["outT"][0]].sem, 1)
                wait_read(act, p, "outT")
                for b in range(2):
                    act.dma_start(out[p, b, 0:640, :].rearrange("(i q) c -> q i c", q=128), o_t[:, 0:5, b, :])\
                       .then_inc(stored.sem, 16)
                    act.dma_start(out[p, b, 640:TV, :], o_t[0:TV - 640, 5, b, :]).then_inc(stored.sem, 16)
                act.wait_ge(stored.sem, stored.at(p, 64))

        @block.vector
        def _(v):
            for tile in (h, xn, tmp1):
                nc.vector.memset(tile[:, T:TP], 0.0).then_inc(dve_made, 1)
            for b in range(2):
                nc.vector.memset(kz[b][:], 0.0).then_inc(dve_made, 1)
            nc.vector.memset(smax[:], 0.0).then_inc(dve_made, 1)
            nc.vector.memset(wb[:, NM - 1], 0.0).then_inc(dve_made, 1)
            nc.vector.memset(eps[:, 0:1], 1e-5).then_inc(dve_made, 1)
            nc.vector.memset(eps[:, 1:2], 1e-6).then_inc(dve_made, 1)
            for n in range(RING):
                nc.vector.memset(work[n][:], 0.0).then_inc(free[n].sem, 1)
            nc.vector.memset(acc[:], 0.0).then_inc(acc_free.sem, 1)
            for n in range(2):
                nc.vector.memset(spare[:, 3 * n:3 * n + 1], 0.0).then_inc(pl_used[n].sem, 1)
                nc.vector.memset(spare[:, 3 * n + 1:3 * n + 2], 0.0).then_inc(p_used.sem, 1)
                nc.vector.memset(spare[:, 3 * n + 2:3 * n + 3], 0.0).then_inc(hid_used.sem, 1)

            v.wait_ge(conv_in, 48)
            steps = [0]

            def trig_link(ins):
                steps[0] += 1
                ins.then_inc(trig_step, 1)
                v.wait_ge(trig_step, steps[0])

            trig_link(nc.vector.tensor_scalar(trig[:, 0, :], phase[:], float(np.pi / 2), None, ALU.add))
            trig_link(nc.vector.tensor_copy(trig[:, 1, :], phase[:]))
            trig_link(nc.vector.tensor_scalar(turns[:], trig[:], float(1 / (2 * np.pi)), ROUND, ALU.mult, ALU.add))
            trig_link(nc.vector.tensor_scalar(turns[:], turns[:], ROUND, None, ALU.subtract))
            trig_link(nc.vector.scalar_tensor_tensor(out=trig[:], in0=turns[:], scalar=-6.28125, in1=trig[:],
                                                     op0=ALU.mult, op1=ALU.add))
            trig_link(nc.vector.scalar_tensor_tensor(out=trig[:], in0=turns[:], scalar=-(2 * np.pi - 6.28125),
                                                     in1=trig[:], op0=ALU.mult, op1=ALU.add))
            trig_link(nc.vector.tensor_scalar(trig[:], trig[:], 3.1415925, -3.1415925, ALU.min, ALU.max))
            assert steps[0] == TRIG_STEPS
            v.wait_ge(sines, 1)
            for tile, n in ((w_real, 0), (w_imag, 1)):
                nc.vector.tensor_tensor(tile, tile, trig[:, n, :].unsqueeze(2).broadcast_to([128, 8, C]),
                                        ALU.mult).then_inc(conv_w, 1)
            v.wait_ge(conv_w, 2)
            nc.vector.tensor_tensor(w_conv[:], w_real, w_imag, ALU.subtract).then_inc(conv_w, 1)
            v.wait_ge(big_in, BIG)
            for n in range(2):
                nc.vector.tensor_copy(w_hi[n][:], raw[n]).then_inc(wsplit, 1)
            v.wait_ge(wsplit, 2)
            for n in range(2):
                nc.vector.tensor_tensor(w_lo[n][:], raw[n], w_hi[n][:].bitcast(f32), ALU.subtract).then_inc(wsplit, 1)
            v.wait_ge(small_in, SMALL)

            with v.Fori(0, PAIRS) as p:
                chain = [0]

                def link(ins):
                    chain[0] += 1
                    ins.then_inc(dve_step.sem, 1)
                    v.wait_ge(dve_step.sem, dve_step.at(p, chain[0]))

                def drained(step, ins):
                    ins.then_inc(free[plan[step][0]].sem, 1)

                wait_full(v, p, "cen1")
                drained("cen1", nc.vector.tensor_copy(halves(cent), slot("cen1")[:, :, 0:HALF]))
                v.wait_ge(rs_ready.sem, rs_ready.at(p, 1))
                nc.vector.tensor_tensor(xn[:, 0:T], cent[:, 0:T], rs[:, 0:T], ALU.mult).then_inc(xn_ready.sem, 1)
                wait_full(v, p, "linq")
                drained("linq", nc.vector.scalar_tensor_tensor(
                    out=halves(tmp1), in0=slot("linq")[:, :, 0:HALF], scalar=lin_b[:, 0:1], in1=halves(q_decay),
                    op0=ALU.add, op1=ALU.mult))
                wait_full(v, p, "link")
                for b in range(2):
                    rows = slice(64 * b, 64 * b + 64)
                    nc.vector.scalar_tensor_tensor(
                        out=halves(kz[b])[rows], in0=slot("link")[rows, :, 0:HALF], scalar=lin_b[rows, 1:2],
                        in1=halves(k_decay)[rows], op0=ALU.add, op1=ALU.mult)\
                      .then_inc(free[plan["link"][0]].sem if b else kz_ready.sem, 1)
                wait_full(v, p, "linv")
                for a in range(2):
                    nc.vector.tensor_tensor(
                        v_lin[:, 3 * a:3 * a + 3, :], slot("linv")[:, a, 0:384].rearrange("p (i c) -> p i c", i=3),
                        lin_vb[:].unsqueeze(1).broadcast_to([128, 3, 128]), ALU.add)\
                      .then_inc(free[plan["linv"][0]].sem if a else vl_ready.sem, 1)
                for n in range(2):
                    v.wait_ge(pl_used[n].sem, pl_used[n].at(p, NB))
                nc.vector.tensor_tensor(halves(h2), acc[:, :, 0:HALF], halves(h), ALU.add).then_inc(acc_free.sem, 1)
                wait_full(v, p, "cen2")
                drained("cen2", nc.vector.tensor_copy(halves(cent), slot("cen2")[:, :, 0:HALF]))
                v.wait_ge(rs_ready.sem, rs_ready.at(p, 2))
                nc.vector.tensor_tensor(x2[:, 0:T], cent[:, 0:T], rs[:, 0:T], ALU.mult).then_inc(x2_ready.sem, 1)
                v.wait_ge(rs_ready.sem, rs_ready.at(p, 3))
                nc.vector.scalar_tensor_tensor(out=xn[:, 0:T], in0=x2[:, 0:T], scalar=ln_ws[:, 0:1],
                                               in1=rs[:, 0:T], op0=ALU.mult, op1=ALU.mult).then_inc(xn_ready.sem, 1)
                wait_full(v, p, "q")
                drained("q", nc.vector.tensor_tensor(halves(tmp1), slot("q")[:, :, 0:HALF], halves(q_cos), ALU.mult))
                wait_full(v, p, "qperm")
                drained("qperm", nc.vector.tensor_tensor(halves(tmp2), slot("qperm")[:, :, 0:HALF], halves(q_sin),
                                                         ALU.mult))
                wait_read(v, p, "qperm")
                link(nc.vector.tensor_tensor(rot[:, 0:T], tmp1[:, 0:T], tmp2[:, 0:T], ALU.add))
                nc.vector.tensor_copy(parts[0][:], rot[:, 0:T]).then_inc(q_parts.sem, 1)
                v.wait_ge(q_parts.sem, q_parts.at(p, 1))
                nc.vector.tensor_tensor(parts[1][:], rot[:, 0:T], parts[0][:].bitcast(f32), ALU.subtract)\
                  .then_inc(q_parts.sem, 1)
                wait_full(v, p, "k")
                link(nc.vector.tensor_tensor(halves(tmp1)[0:64], slot("k")[0:64, :, 0:HALF], halves(k_tab)[0:64],
                                             ALU.mult))
                drained("k", nc.vector.tensor_tensor(halves(tmp2)[0:64], slot("k")[64:128, :, 0:HALF],
                                                     halves(k_tab)[64:128], ALU.mult))
                wait_read(v, p, "k")
                link(nc.vector.tensor_tensor(rot[0:64, 0:T], tmp1[0:64, 0:T], tmp2[0:64, 0:T], ALU.add))
                nc.vector.tensor_copy(kparts[0][:], rot[0:64, 0:T]).then_inc(k_parts.sem, 1)
                v.wait_ge(k_parts.sem, k_parts.at(p, 1))
                nc.vector.tensor_tensor(kparts[1][:], rot[0:64, 0:T], kparts[0][:].bitcast(f32), ALU.subtract)\
                  .then_inc(k_parts.sem, 1)
                for b in range(2):
                    for n, (i, w, heads) in enumerate(score_rounds()):
                        step, m = ("max", b, n), ROWS[i]
                        wait_full(v, p, step)
                        to = smax[0:m, i, heads[0]:heads[-1] + 1]
                        src, axis = slot(step)[0:m, 0:2, 0:w // 2], AX.XY
                        if w == 128:
                            src, axis = slot(step)[0:m, 0, 0:NH * w].rearrange("p (g s) -> p g s", g=NH), AX.X
                        elif w == 256:
                            src, axis = slot(step)[0:m].rearrange("p a (g s) -> p (a g) s", g=2), AX.X
                        elif w <= 512:
                            src, axis = slot(step)[0:m, 0:2, 0:w], AX.X
                        drained(step, nc.vector.tensor_reduce(to, src, axis, ALU.max))
                    wait_read(v, p, ("max", b, len(score_rounds()) - 1))
                    if b:
                        wait_full(v, p, ("negmax", 0))
                    link(nc.vector.tensor_scalar(nmh[:], smax[:], -1.0, None, ALU.mult))
                    nc.vector.tensor_copy(nmx[:, :, :, 0], nmh[:].bitcast(f32)).then_inc(nm_ready.sem, 1)
                    nc.vector.scalar_tensor_tensor(out=nmx[:, :, :, 1], in0=smax[:], scalar=-1.0,
                                                   in1=nmh[:].bitcast(f32), op0=ALU.mult, op1=ALU.subtract)\
                      .then_inc(nm_ready.sem, 1)
                for b in range(2):
                    rows = slice(64 * b, 64 * b + 64)
                    v.wait_ge(rd_ready.sem, rd_ready.at(p, b + 1))
                    nc.vector.tensor_tensor(xn[:, 0:T], cent[:, 0:T], rs[:, 0:T], ALU.mult).then_inc(yn_ready.sem, 1)
                    wait_full(v, p, ("wo", b))
                    drained(("wo", b), nc.vector.tensor_tensor(
                        halves(x2)[rows], slot(("wo", b))[rows, :, 0:HALF], halves(x2)[rows], ALU.add))
                v.wait_ge(rs_ready.sem, rs_ready.at(p, 4))
                nc.vector.scalar_tensor_tensor(out=flat[:, 0:T], in0=x2[:, 0:T], scalar=ln_ws[:, 1:2],
                                               in1=rs[:, 0:T], op0=ALU.mult, op1=ALU.mult).then_inc(flat_ready.sem, 1)

                def over_experts(stat):
                    return stat[:].unsqueeze(2).broadcast_to([128, 2 * NB, NE])

                ranks = rank_t[:].unsqueeze(1).broadcast_to([128, 2 * NB, NE])
                logits = slot("router")[:, 0, 0:2 * NB * NE].rearrange("p (g e) -> p g e", e=NE)
                wait_full(v, p, "router")
                link(nc.vector.tensor_reduce(s1[:], logits, AX.X, ALU.max))
                drained("router", nc.vector.tensor_tensor(lg[:], logits, over_experts(s1), ALU.subtract))
                for b in range(2):
                    rows, other = slice(64 * b, 64 * b + 64), slice(64 - 64 * b, 128 - 64 * b)
                    v.wait_ge(xhi_ready.sem, xhi_ready.at(p, b + 1))
                    nc.vector.tensor_tensor(xs[b][other], flat[rows, 0:T], xs[b][rows].bitcast(f32), ALU.subtract)\
                      .then_inc(xlo_ready.sem, 1)
                v.wait_ge(lge_ready.sem, lge_ready.at(p, 1))
                link(nc.vector.tensor_reduce(s1[:], ta[:], AX.X, ALU.add))
                link(nc.vector.reciprocal(s2[:], s1[:]))
                link(nc.vector.tensor_tensor(lg[:], ta[:], over_experts(s2), ALU.mult))

                def first_largest(src, top, pick):
                    link(nc.vector.tensor_reduce(top[:], src[:], AX.X, ALU.max))
                    link(nc.vector.tensor_tensor(tb[:], src[:], over_experts(top), ALU.is_equal))
                    link(nc.vector.tensor_tensor(tb[:], tb[:], ranks, ALU.mult))
                    link(nc.vector.tensor_reduce(s3[:], tb[:], AX.X, ALU.max))
                    link(nc.vector.tensor_tensor(pick[:], tb[:], over_experts(s3), ALU.is_equal))

                first_largest(lg, s1, oh)
                link(nc.vector.scalar_tensor_tensor(out=ta[:], in0=oh[:], scalar=-2.0, in1=lg[:],
                                                    op0=ALU.mult, op1=ALU.add))
                first_largest(ta, s2, tb)
                link(nc.vector.tensor_tensor(oh[:], oh[:], tb[:], ALU.add))
                link(nc.vector.tensor_tensor(oh[:], oh[:], lg[:], ALU.mult))
                link(nc.vector.scalar_tensor_tensor(out=s1[:], in0=s1[:], scalar=1e-9, in1=s2[:],
                                                    op0=ALU.add, op1=ALU.add))
                link(nc.vector.reciprocal(s3[:], s1[:]))
                nc.vector.tensor_tensor(ta[:], oh[:], over_experts(s3), ALU.mult).then_inc(rw_ready.sem, 1)

                def weigh(n):
                    c, m, b = n // (2 * NM), n // 2 % NM, n % 2
                    wait_read(v, p, ("moe", c, m, b))
                    if not b:
                        count = (c + 1) * 32 * len(segments[m])
                        v.wait_ge(wb_in[m].sem, wb_in[m].at(p, count))
                    nc.vector.tensor_tensor(hid[n % 4], hid[n % 4], wb[:, m, b, :], ALU.mult)\
                      .then_inc(hid_ready.sem, 1)

                for n in range(4 * NM):
                    step = ("moe", n // (2 * NM), n // 2 % NM, n % 2)
                    v.wait_ge(gate_ready.sem, gate_ready.at(p, n + 1))
                    v.wait_ge(hid_used.sem, hid_used.at(p, (n - 4) // 2 + 1))
                    drained(step, nc.vector.tensor_tensor(hid[n % 4], slot(step)[:, 1, 0:HALF], gate[n % 4],
                                                          ALU.mult))
                    if n:
                        weigh(n - 1)
                weigh(4 * NM - 1)
                v.wait_ge(base_ready.sem, base_ready.at(p, 1))
                for c in range(2):
                    v.wait_ge(hid_used.sem, hid_used.at(p, NM * (c + 1)))
                    nc.vector.tensor_tensor(halves(fin)[:, c], acc[:, c, 0:HALF], halves(h2)[:, c], ALU.add)\
                      .then_inc(acc_free.sem if c else fin_ready.sem, 1)
                assert chain[0] == DVE_STEPS, chain[0]

        @block.tensor
        def _(pe):
            pe.wait_ge(conv_w, 3)
            pe.wait_ge(small_in, SMALL)
            pe.wait_ge(wsplit, 4)
            pe.wait_ge(big_in, BIG)
            pe.wait_ge(pool_made, POOL_MADE)
            pe.wait_ge(dve_made, DVE_MADE)

            def mix(p, step, weights, src):
                wait_free(pe, p, step)
                for a in range(2):
                    last = nc.tensor.matmul(slot(step)[0:weights.shape[1], a, 0:HALF], weights, halves(src)[:, a],
                                            start=True, stop=True)
                last.then_inc(full[plan[step][0]].sem, 1)

            def spans(j):
                return [(a, max(128 * j, a * HALF), (a + 1) * HALF) for a in range(2) if 128 * j < (a + 1) * HALF]

            with pe.Fori(0, PAIRS) as p:
                wait_free(pe, p, "conv")
                pe.wait_ge(x_loaded.sem, x_loaded.at(p, 64))
                for a in range(2):
                    for j in range(TAPS // 2):
                        for b in range(2):
                            last = nc.tensor.matmul(slot("conv")[64 * b:64 * b + 64, a, 0:HALF], w_conv[:, j, :],
                                                    x_in[:, b, 2 * j + HALF * a:2 * j + HALF * (a + 1)],
                                                    start=(j == 0), stop=(j == TAPS // 2 - 1))
                last.then_inc(full[plan["conv"][0]].sem, 1)
                wait_read(pe, p, "conv")
                mix(p, "cen1", center[:], h)
                pe.wait_ge(sq_ready.sem, sq_ready.at(p, 1))
                mix(p, "var1", average[:], sq)
                pe.wait_ge(xn_ready.sem, xn_ready.at(p, 1))
                mix(p, "linq", lin_ws[:, 0, :], xn)
                mix(p, "link", lin_ws[:, 1, :], xn)
                wait_free(pe, p, "linv")
                for i in range(NB):
                    last = nc.tensor.matmul(slot("linv")[:, i // 3, 128 * (i % 3):128 * (i % 3) + 128],
                                            xn[:, 128 * i:128 * i + 128], lin_ws[:, 2, :], start=True, stop=True)
                last.then_inc(full[plan["linv"][0]].sem, 1)

                wait_read(pe, p, "linq")
                pe.wait_ge(kz_ready.sem, kz_ready.at(p, 1))
                wait_read(pe, p, "link")

                def lin_values(j):
                    for b in range(2):
                        pe.wait_ge(pl_masked.sem, pl_masked.at(p, 2 * j + b + 1))
                        for a, t0, t1 in spans(j):
                            last = nc.tensor.matmul(acc[64 * b:64 * b + 64, a, t0 - a * HALF:t1 - a * HALF],
                                                    v_lin[0:ROWS[j], j, 64 * b:64 * b + 64],
                                                    p_lin[b][0:ROWS[j], t0 - 128 * j:t1 - 128 * j],
                                                    start=(j == 0), stop=(j == NB - 1 or (a == 0 and j == 2)))
                        last.then_inc(pl_used[b].sem, 1)

                for j in range(NB):
                    for b in range(2):
                        step = ("lin", j, b)
                        wait_free(pe, p, step)
                        for n, (o, w) in enumerate(pieces(WIDTH[j])):
                            last = nc.tensor.matmul(slot(step)[0:ROWS[j], n, 0:w], kz[b][:, 128 * j:128 * j + ROWS[j]],
                                                    tmp1[:, 128 * j + o:128 * j + o + w], start=True, stop=True)
                        last.then_inc(full[plan[step][0]].sem, 1)
                    if j == 1:
                        pe.wait_ge(vl_ready.sem, vl_ready.at(p, 1))
                        wait_read(pe, p, "linv")
                        pe.wait_ge(acc_free.sem, acc_free.at(p, 0))
                    if j:
                        lin_values(j - 1)
                lin_values(NB - 1)
                pe.wait_ge(acc_free.sem, acc_free.at(p, 1))
                mix(p, "cen2", center[:], h2)
                pe.wait_ge(sq_ready.sem, sq_ready.at(p, 2))
                mix(p, "var2", average[:], sq)
                pe.wait_ge(sq_ready.sem, sq_ready.at(p, 3))
                mix(p, "ms1", average[:], sq)
                pe.wait_ge(xn_ready.sem, xn_ready.at(p, 2))
                for n, step in enumerate(("q", "qperm", "k")):
                    mix(p, step, qkv_ws[:, 128 * n:128 * n + 128], xn)
                wait_free(pe, p, "v")
                for i in range(NB):
                    last = nc.tensor.matmul(slot("v")[:, 0, 64 * i:64 * i + 64], xn[:, 128 * i:128 * i + 128],
                                            qkv_ws[:, 384:448], start=True, stop=True)
                last.then_inc(full[plan["v"][0]].sem, 1)

                for b in range(2):
                    pe.wait_ge(stacks[b].sem, stacks[b].at(p, 16 * 9))
                    for n, (i, w, heads) in enumerate(score_rounds()):
                        step, m = ("max", b, n), ROWS[i]
                        wait_free(pe, p, step)
                        for g, hh in enumerate(heads):
                            cut = pieces(w)
                            for k, (o, cw) in enumerate(cut):
                                if w == 128:
                                    bank, col = 0, g * w
                                elif w == 256:
                                    bank, col = g // 2, g % 2 * w
                                else:
                                    bank, col = g + k, 0
                                diag = k == len(cut) - 1
                                nc.tensor.matmul(slot(step)[0:m, bank, col:col + cw],
                                                 qs[b][:, hh, 128 * i:128 * i + m], ks[b][:, hh // 2, o:o + cw],
                                                 start=True, stop=not diag)
                                if diag:
                                    last = nc.tensor.matmul(slot(step)[0:m, bank, col + cw - m:col + cw],
                                                            eye_b[:, 0:m], neg_qk[:, 0:m], start=False, stop=True)
                        last.then_inc(full[plan[step][0]].sem, 1)
                    step = ("negmax", b)
                    pe.wait_ge(nm_ready.sem, nm_ready.at(p, 2 * b + 2))
                    wait_free(pe, p, step)
                    for i in range(NB):
                        last = nc.tensor.matmul(slot(step)[0:2 * NH, i // 3, 128 * (i % 3):128 * (i % 3) + 128],
                                                nmx[0:ROWS[i], i].rearrange("p h n -> p (h n)"),
                                                ident[0:ROWS[i], :], start=True, stop=True)
                    last.then_inc(full[plan[step][0]].sem, 1)

                pe.wait_ge(v_ready.sem, v_ready.at(p, 1))
                wait_read(pe, p, "v")
                for b in range(2):
                    pe.wait_ge(m_in.sem, m_in.at(p, 64 * (b + 1)))

                    def values(j):
                        for hh in range(NH):
                            n = NH * j + hh
                            wait_read(pe, p, ("score", b, j, hh))
                            for a, t0, t1 in spans(j):
                                last = nc.tensor.matmul(
                                    acc[32 * hh:32 * hh + 32, a, t0 - a * HALF:t1 - a * HALF],
                                    v_aug[b][0:ROWS[j], j, hh // 2, :],
                                    pt[n % PT][0:ROWS[j], t0 - 128 * j:t1 - 128 * j],
                                    start=(j == 0), stop=(j == NB - 1 or (a == 0 and j == 2)))
                        last.then_inc(p_used.sem, 1)

                    for j in range(NB):
                        for hh in range(NH):
                            step = ("score", b, j, hh)
                            wait_free(pe, p, step)
                            for n, (o, w) in enumerate(pieces(WIDTH[j])):
                                last = nc.tensor.matmul(slot(step)[0:ROWS[j], n, 0:w],
                                                        ks[b][:, hh // 2, 128 * j:128 * j + ROWS[j]],
                                                        qs[b][:, hh, 128 * j + o:128 * j + o + w],
                                                        start=True, stop=(n > 0))
                            last = nc.tensor.matmul(slot(step)[0:ROWS[j], 0, 0:ROWS[j]], eye_b[:, 0:ROWS[j]],
                                                    neg_kq[:, 0:ROWS[j]], start=False, stop=True)
                            last.then_inc(full[plan[step][0]].sem, 1)
                            if j and hh == 1:
                                if j == 1:
                                    pe.wait_ge(acc_free.sem, acc_free.at(p, b + 1))
                                values(j - 1)
                    values(NB - 1)
                    pe.wait_ge(acc_free.sem, acc_free.at(p, b + 2))
                    mix(p, ("den", b), den_sel[:], cent)
                    step = ("wo", b)
                    wait_free(pe, p, step)
                    pe.wait_ge(yn_ready.sem, yn_ready.at(p, b + 1))
                    for a in range(2):
                        last = nc.tensor.matmul(slot(step)[64 * b:64 * b + 64, a, 0:HALF], wo_ws[:], halves(xn)[:, a],
                                                start=True, stop=True)
                    last.then_inc(full[plan[step][0]].sem, 1)

                pe.wait_ge(sq_ready.sem, sq_ready.at(p, 4))
                mix(p, "ms2", average[:], sq)
                pe.wait_ge(flat_ready.sem, flat_ready.at(p, 1))
                wait_free(pe, p, "router")
                for i in range(NB):
                    last = nc.tensor.matmul(slot("router")[:, 0, 2 * NE * i:2 * NE * (i + 1)],
                                            flat[:, 128 * i:128 * i + 128], router_ws[:], start=True, stop=True)
                last.then_inc(full[plan["router"][0]].sem, 1)
                pe.wait_ge(rw_ready.sem, rw_ready.at(p, 1))
                wait_free(pe, p, "rwT")
                for i in range(NB):
                    last = nc.tensor.matmul(slot("rwT")[0:2 * NE, i // 3, 128 * (i % 3):128 * (i % 3) + 128],
                                            ta[:, 2 * i:2 * i + 2, :].rearrange("p b e -> p (b e)"), ident[:],
                                            start=True, stop=True)
                last.then_inc(full[plan["rwT"][0]].sem, 1)

                pe.wait_ge(xhi_ready.sem, xhi_ready.at(p, 2))
                pe.wait_ge(xlo_ready.sem, xlo_ready.at(p, 2))
                pe.wait_ge(acc_free.sem, acc_free.at(p, 3))

                def down(n):
                    c, m = n // NM, n % NM
                    for b in range(2):
                        pe.wait_ge(hid_ready.sem, hid_ready.at(p, 2 * n + b + 1))
                        last = nc.tensor.matmul(acc[64 * b:64 * b + 64, c, 0:HALF], w2_ws[:, m, :],
                                                hid[(2 * n + b) % 4], start=(m == 0), stop=(m == NM - 1))
                    return last

                for n in range(2 * NM):
                    c, m = n // NM, n % NM
                    for b in range(2):
                        step = ("moe", c, m, b)
                        wait_free(pe, p, step)
                        for k in range(2):
                            for part in (w_hi, w_lo):
                                last = nc.tensor.matmul(slot(step)[:, k, 0:HALF], part[k][:, 128 * m:128 * m + 128],
                                                        halves(xs[b])[:, c], start=(part is w_hi), stop=(part is w_lo))
                        last.then_inc(full[plan[step][0]].sem, 1)
                    if n:
                        down(n - 1).then_inc(hid_used.sem, 1)
                down(2 * NM - 1).then_inc(hid_used.sem, 1)

                wait_free(pe, p, "outT")
                pe.wait_ge(fin_ready.sem, fin_ready.at(p, 1))
                pe.wait_ge(acc_free.sem, acc_free.at(p, 4))
                for i in range(NB):
                    last = nc.tensor.transpose(slot("outT")[:, i // 3, 128 * (i % 3):128 * (i % 3) + 128],
                                               fin[:, 128 * i:128 * i + 128], ident[:])
                last.then_inc(full[plan["outT"][0]].sem, 1)


_OUT = (B, TV, C)


def _layouts(inputs):
    f = np.float32
    a = {k: np.asarray(v) for k, v in inputs.items()}

    def twice(w):
        z = np.zeros((2 * w.shape[0], 2 * w.shape[1]), f)
        z[:w.shape[0], :w.shape[1]] = w
        z[w.shape[0]:, w.shape[1]:] = w
        return z

    got = {}
    x = np.zeros((PAIRS, 2, C, XW), f)
    x[..., :S_IN] = a["x"].transpose(0, 2, 1).reshape(PAIRS, 2, C, S_IN)
    got["xT"] = x
    for name, key in (("wr", "L0_tok_w_real"), ("wi", "L0_tok_w_imag")):
        w = a[key].transpose(2, 1, 0).reshape(TAPS // 2, 2, C, C)
        got[name] = w.transpose(1, 2, 0, 3).reshape(128, -1)
    got["ph"] = np.repeat(a["L0_tok_phases"].reshape(TAPS // 2, 2).T, 64, axis=0)
    w, bias = a["L0_attn_Wqkv"], a["L0_attn_bqkv"]
    got["lin_w"] = np.stack([twice(w[:, 64 * n:64 * n + 64]) for n in range(3)], axis=1)
    got["lin_bqk"] = np.stack([np.tile(bias[64 * n:64 * n + 64], 2) for n in range(2)], axis=1)
    got["lin_bv"] = np.broadcast_to(np.tile(bias[128:192], 2), (128, 128))
    got["ln_w"] = np.stack([np.tile(a["L0_ffn_ln1_w"], 2), np.tile(a["L0_ffn_ln2_w"], 2)], axis=1)
    d = np.arange(64)
    partner = d // HD * HD + (d % HD + HD // 2) % HD
    wq, wk, wv = (a[f"L0_ffn_{n}"] for n in ("wq", "wk", "wv"))
    got["qkv_w"] = np.concatenate([twice(wq.T), twice(wq[partner].T), twice(wk.T), twice(wk[partner[:32]].T),
                                   twice(wv.T)], axis=1)
    wo = np.zeros((NH, 32, C), f)
    wo[:, :HD] = a["L0_ffn_wo"].T.reshape(NH, HD, C)
    got["wo_w"] = wo.reshape(128, C)
    got["router_w"] = twice(a["L0_ffn_router_w"].T)
    for name, key in (("w1T", "L0_ffn_w1"), ("w3T", "L0_ffn_w3")):
        w = np.zeros((2, C, MP), f)
        w[:, :, :NE * HID] = a[key].transpose(2, 0, 1).reshape(C, NE * HID)
        got[name] = w.reshape(128, MP)
    w = np.zeros((MP, C), f)
    w[:NE * HID] = a["L0_ffn_w2"].transpose(0, 2, 1).reshape(NE * HID, C)
    got["w2T"] = w.reshape(NM, 128, C).transpose(1, 0, 2).reshape(128, -1)
    got["eye"] = np.eye(128, dtype=f)
    got["cen"] = twice(np.eye(64, dtype=f) - f(1 / 64))
    got["avg"] = twice(np.full((64, 64), 1 / 64, f))
    sel = np.zeros((128, 128), f)
    for hh in range(NH):
        sel[32 * hh + HD, 32 * hh:32 * hh + 32] = 1
    got["dsel"] = sel
    t = np.arange(T)
    got["qdec"] = np.broadcast_to((ALPHA ** t / 8).astype(f), (128, T))
    got["kdec"] = np.broadcast_to((ALPHA ** -t.astype(np.float64)).astype(f), (128, T))
    inv = (1.0 / 10000.0 ** (np.arange(0, HD, 2, dtype=f) / HD)).astype(f)
    angle = np.outer(t.astype(f), inv).astype(f)
    cos = np.tile(np.cos(angle), (1, 2)).T.astype(f)
    sin = np.concatenate([-np.sin(angle), np.sin(angle)], axis=1).T.astype(f)
    got["qcos"] = np.tile(cos, (8, 1)) * f(HD ** -0.5)
    got["qsin"] = np.tile(sin, (8, 1)) * f(HD ** -0.5)
    got["ktab"] = np.concatenate([np.tile(cos, (4, 1)), np.tile(sin, (4, 1))])
    got["rank"] = np.broadcast_to(np.arange(NE, 0, -1).astype(f), (128, NE))
    got["mask01"] = np.triu(np.ones((128, 128), f))
    return {k: np.ascontiguousarray(v) for k, v in got.items()}


def kernel(**inputs):
    import concourse.bacc as bacc
    from concourse.bass_utils import run_bass_kernel_spmd

    nc = bacc.Bacc("TRN2", target_bir_lowering=False, num_devices=1)
    arrays = _layouts(inputs)
    args = {k: nc.dram_tensor(f"in_{k}", v.shape, mybir.dt.from_np(v.dtype), kind="ExternalInput").ap()
            for k, v in arrays.items()}
    out = nc.dram_tensor("out_layer", _OUT, mybir.dt.float32, kind="ExternalOutput").ap()
    audio_tower(nc, **args, out=out.rearrange("(p b) t c -> p b t c", b=2))
    r = run_bass_kernel_spmd(nc, [{f"in_{k}": v for k, v in arrays.items()}], core_ids=[0])
    return r.results[0]["out_layer"]
```

```python
from contextlib import ExitStack
from itertools import product

import numpy as np

import concourse.bass as bass
from concourse import mybir

B, S_IN, C, TAPS = 4, 750, 64, 16
TV = S_IN - TAPS + 1
T = TV + TV % 2
TP = 768
HALF = T // 2
PAIRS = B // 2
NB = (T + 127) // 128
WIDTH = [T - 128 * j for j in range(NB)]
ROWS = [min(128, w) for w in WIDTH]
NH, NKV, HD = 4, 2, 16
NE, HID = 8, int(8 / 3 * C)
NM = (NE * HID + 127) // 128
MP = NM * 128
XW = S_IN + 1
ALPHA = float(np.float32(0.99))
NEG = -1e30
BANKS = 6
TRIG_STEPS = 7
ROUND = 12582912.0
PT = 8
SETS = 3
TOP_STEPS = 11
POOL_TAKES = 4
LAG = 2


def pieces(width):
    return [(0, width)] if width <= 512 else [(0, width // 2), (width // 2, width // 2)]


def spans(j):
    return [(a, max(128 * j, a * HALF), (a + 1) * HALF) for a in range(2) if 128 * j < (a + 1) * HALF]


def score_rounds():
    out = []
    for i in range(NB):
        w = min(128 * (i + 1), T)
        n = {128: 4, 256: 4, 384: 2, 512: 2}.get(w, 1)
        out += [(i, w, tuple(range(h, h + n))) for h in range(0, NH, n)]
    return out


ROUNDS = score_rounds()


ORDER = """
conv 0 0-1, conv 1 0, cen1 0, var1 0, conv 1 1, linq 0, link 0, cen1 1, linv 0, lin 0 0 0, var1 1, lin 0 0 1
lin 0 1 0-1, lv 0 0, lin 0 2 0-1, lv 0 1, lin 0 3 0-1, lv 0 2, lin 0 4 0-1, lv 0 3, lin 0 5 0-1, lv 0 4-5, h2 0
linq 1, cen2 0, link 1, var2 0, linv 1, lin 1 0 0-1, ms1 0, lin 1 1 0-1, lv 1 0, lin 1 2 0-1, q 0, qperm 0
lv 1 1, k 0, lin 1 3 0-1, lv 1 2, lin 1 4 0-1, lv 1 3, lin 1 5 0-1, lv 1 4-5, v 0, h2 1, cen2 1, var2 1
max 0 0-5, ms1 1, max 0 6-7, q 1, max 0 8-13, qperm 1, negmax 0, max 1 0, k 1, max 1 1, v 1, max 1 2
score 0 0 0, max 1 3-4, score 0 0 1, max 1 5-6, score 0 0 2, max 1 7-9, score 0 0 3, score 0 1 0, max 1 10
score 0 1 1, max 1 11, pv 0 0, score 0 1 2, max 1 12, score 0 1 3, score 0 2 0, max 1 13, pv 0 1, score 0 2 1-3
score 0 3 0, negmax 1, score 0 3 1, max 2 0, score 0 3 2-3, max 2 1, pv 0 2, max 2 2, score 0 4 0, max 2 3
score 0 4 1, max 2 4, score 0 4 2, max 2 5, pv 0 3, score 0 4 3, score 0 5 0, pv 0 4, score 0 5 1-3, max 2 6
score 1 0 0, max 2 7, pv 0 5, y 0, score 1 0 1, max 2 8, score 1 0 2, max 2 9, score 1 0 3, den 0, max 2 10
score 1 1 0, max 2 11, pv 1 0, score 1 1 1, wo 0, score 1 1 2, max 2 12-13, score 1 1 3, score 1 2 0, pv 1 1
score 1 2 1-3, negmax 2, score 1 3 0, max 3 0, score 1 3 1-2, max 3 1, pv 1 2, score 1 3 3, max 3 2, score 1 4 0
max 3 3, pv 1 3, max 3 4, score 1 4 1-2, max 3 5, score 1 4 3, score 1 5 0-2, pv 1 4, max 3 6, score 1 5 3
max 3 7, pv 1 5, y 1, score 2 0 0-2, den 1, max 3 8, score 2 0 3, score 2 1 0-1, pv 2 0, wo 1, score 2 1 2
max 3 9-10, score 2 1 3, score 2 2 0, pv 2 1, score 2 2 1-3, max 3 11, pv 2 2, max 3 12, score 2 3 0-3, max 3 13
score 2 4 0-3, pv 2 3-4, score 2 5 0, negmax 3, score 2 5 1-3, ms2 0, pv 2 5, y 2, score 3 0 0-1, den 2
score 3 0 2-3, score 3 1 0, pv 3 0, wo 2, score 3 1 1, router 0, top 0 0, score 3 1 2-3, top 0 1, score 3 2 0-3
pv 3 1, top 0 2-3, score 3 3 0-1, pv 3 2, score 3 3 2-3, top 0 4, split 0, top 0 5, split 1, top 0 6
score 3 4 0-1, top 0 7, score 3 4 2-3, pv 3 3, score 3 5 0, top 0 8-10, score 3 5 1, rwT 0, xlo 0 1, score 3 5 2
xlo 0 0, pv 3 4, score 3 5 3, split 2-3, pv 3 5, y 3, moe 0 0 0 0-1, moe 0 0 1 0, den 3, wo 3, moe 0 0 1 1
moe 0 0 2 0-1, ms2 1, moe 0 0 3-5 0-1, router 1, top 1 0-3, moe 0 0 6 0-1, top 1 4, moe 0 0 7 0-1, top 1 5
moe 0 0 8 0-1, top 1 6, moe 0 0 9 0, top 1 7, moe 0 0 9 1, top 1 8-9, moe 0 0 10 0, top 1 10, moe 0 0 10 1
xlo 1 0, moe 0 1 0 0, rwT 1, moe 0 1 0 1, moe 0 1 1 0-1, fin 0 0, moe 0 1 2-4 0-1, moe 0 1 5 0, xlo 1 1
moe 0 1 5 1, moe 0 1 6-10 0-1, moe 1 0 0-3 0-1, fin 0 1, moe 1 0 4-6 0-1, outT 0, moe 1 0 7-10 0-1
moe 1 1 0-4 0-1, fin 1 0, moe 1 1 5-10 0-1, last, fin 1 1, outT 1
"""


def schedule():
    out = []
    for entry in ORDER.replace("\n", ",").split(","):
        if entry:
            kind, *at = entry.split()
            ends = [[int(end) for end in n.split("-")] for n in at]
            out += [(kind, *n) for n in product(*(range(e[0], e[-1] + 1) for e in ends))]
    return out


UNSLOTTED = ("xlo", "top", "split", "lv", "h2", "pv", "y", "fin", "last")
STEPS = schedule()


def wide(step):
    if step[0] in ("lin", "score"):
        return WIDTH[step[2]] > 512
    if step[0] == "max":
        return step[2] > 0
    return step[0] not in ("conv", "v", "router")


def slot_plan():
    plan, last, uses, at = {}, {}, [0] * BANKS, 0
    for step in STEPS:
        if step[0] not in UNSLOTTED:
            if wide(step):
                at += at % 2
            banks = [(at + n) % BANKS for n in range(1 + wide(step))]
            before = {last[bank] for bank in banks if bank in last}
            plan[step] = banks[0], uses[banks[0]], sorted(before, key=STEPS.index)
            uses[banks[0]] += 1
            for bank in banks:
                last[bank] = step
            at = (at + len(banks)) % BANKS
    return plan


def audio_tower(nc, xT, wr, wi, ph, lin_w, lin_bqk, lin_bv, ln_w, qkv_w, wo_w, router_w,
                w1T, w3T, w2T, eye, cen, avg, dsel, qdec, kdec, qcos, qsin, ktab, rank, mask01, out):
    f32, f32r, bf16 = mybir.dt.float32, mybir.dt.float32r, mybir.dt.bfloat16
    ALU, ACT, AX = mybir.AluOpType, mybir.ActivationFunctionType, mybir.AxisListType

    q_scr = nc.dram_tensor("q_scratch", [PAIRS, 2, 2, NH, HD, T], f32).ap()
    k_scr = nc.dram_tensor("k_scratch", [PAIRS, 2, 2, NKV, HD, T], f32).ap()
    w_scr = nc.dram_tensor("route_scratch", [PAIRS, 2, NE, T], f32).ap()

    with ExitStack() as ctx:
        def sb(name, shape, dt=f32):
            return ctx.enter_context(nc.sbuf_tensor(name, shape, dt))

        def once(name):
            return ctx.enter_context(nc.semaphore(name))

        phase = sb("phase", [128, 8])
        trig = sb("trig", [128, 2, 8])
        turns = sb("turns", [128, 2, 8])
        lin_ws = sb("lin_ws", [128, 3, 128])
        lin_b = sb("lin_b", [128, 2])
        lin_vb = sb("lin_vb", [128, 128])
        ln_ws = sb("ln_ws", [128, 2])
        qkv_ws = sb("qkv_ws", [128, 3 * 128 + 64])
        wo_ws = sb("wo_ws", [128, C])
        router_ws = sb("router_ws", [128, 2 * NE])
        w_split = sb("w_split", [128, 4 * MP], f32r)
        w_hi, w_lo = ([w_split[:, n * MP:(n + 1) * MP] for n in pair] for pair in ((0, 1), (2, 3)))
        w2_ws = sb("w2_ws", [128, NM, C])
        ident = sb("ident", [128, 128])
        center = sb("center", [128, 128])
        average = sb("average", [128, 128])
        den_sel = sb("den_sel", [128, 128])
        q_decay = sb("q_decay", [128, T])
        k_decay = sb("k_decay", [128, T])
        q_cos = sb("q_cos", [128, T])
        q_sin = sb("q_sin", [128, T])
        k_tab = sb("k_tab", [128, T])
        rank_t = sb("rank_t", [128, NE])
        keep01 = sb("keep01", [128, 128])
        eye_b = sb("eye_b", [128, 128], bf16)
        neg_qk = sb("neg_qk", [128, 128], bf16)
        neg_kq = sb("neg_kq", [128, 128], bf16)
        eps = sb("eps", [128, 2])

        wb_space = sb("wb_space", [128, NM, T])
        wb = wb_space[:].rearrange("p m (b t) -> p m b t", b=2)

        first_space = sb("first_space", [128, 8, T])
        cent, tmp2, rs, xn, sq, tmp1, kza, kzb = ([space[:, n, :] for space in (first_space, wb_space)]
                                                  for n in range(8))
        kz = list(zip(kza, kzb))
        x_in = [space[:, n:n + 3, :].rearrange("p m t -> p (m t)")[:, 0:2 * XW].rearrange("p (b t) -> p b t", b=2)
                for space, n in ((first_space, 2), (wb_space, 8))]
        h = [sb(f"h{g}", [128, TP])[:] for g in range(PAIRS)]
        h2 = [sb(f"h2_{g}", [128, T])[:] for g in range(PAIRS)]
        x2 = [sb(f"x2_{g}", [128, T])[:] for g in range(PAIRS)]
        v_lin = [sb(f"v_lin{g}", [128, NB, 128])[:] for g in range(PAIRS)]
        parts = [[sb(f"part{g}{n}", [128, T], f32r) for n in range(2)] for g in range(PAIRS)]
        kparts = [sb(f"kpart{n}", [64, T], f32r) for n in range(2)]
        qs = [sb(f"qs{b}", [128, NH, T], f32r)[:] for b in range(2)]
        ks = [sb(f"ks{b}", [128, NKV, T], f32r)[:] for b in range(2)]
        qs.append(w_split[:, 0:NH * T].rearrange("p (h t) -> p h t", h=NH))
        ks.append(w_split[:, NH * T:(NH + NKV) * T].rearrange("p (h t) -> p h t", h=NKV))
        v_aug = [sb(f"v_aug{b}", [128, NB, NKV, 32]) for b in range(B)]
        smax = sb("smax", [128, NB, NH])
        nmx = sb("nmx", [128, NB, NH, 2])
        nmh = sb("nmh", [128, NB, NH], f32r)
        exps = sb("exps", [128, PT, T])
        pt = [exps[:, n, :] for n in range(PT)]
        lg, ta, tb, oh = (sb(n, [128, 2 * NB, NE]) for n in ("lg", "ta", "tb", "oh"))
        s1, s2, s3 = (sb(n, [128, 2 * NB]) for n in ("s1", "s2", "s3"))
        raw = [first_space[:, n:n + 2].rearrange("p a t -> p (a t)")[:, 0:MP] for n in (4, 6)]
        w_real, w_imag, w_conv = (pt[n][:, 0:8 * C].rearrange("p (j c) -> p j c", c=C) for n in (4, 5, 6))
        p_lin = pt[4:6]
        rot, krot, fin, xs, flat = sq, [tile[0:64] for tile in cent], h, parts, h[1]
        ysb, rden, yn, rs2 = cent[0], rs[0], xn[0], tmp2[0]
        nrow = v_lin[0].rearrange("p i c -> p (i c)")[0:2 * NH]
        r_wT = v_lin[1].rearrange("p i c -> p (i c)")[0:2 * NE]
        gate = [(q_cos, q_sin)[n // 2][:, n % 2 * HALF:(n % 2 + 1) * HALF] for n in range(4)]
        hid = [pt[n // 2][:, n % 2 * HALF:(n % 2 + 1) * HALF] for n in range(2 * (LAG + 1))]
        o_t = v_lin

        work = ctx.enter_context(nc.psum_tensor("work", [128, BANKS, 512], f32))
        acc = ctx.enter_context(nc.psum_tensor("acc", [128, 2, 512], f32))

        plan = slot_plan()
        full = [once(f"full{n}") for n in range(BANKS)]
        free = [once(f"free{n}") for n in range(BANKS)]
        ACC_OUT = {("h2", 0): 1, ("h2", 1): 2, **{("y", bt): 3 + bt for bt in range(B)},
                   **{("fin", g, c): 7 + 2 * g + c for g in range(PAIRS) for c in range(2)}}
        acc_out = once("acc_out")
        squared = {k: once(f"squared_{k}") for k in ("var1", "var2", "ms1", "ms2")}
        rooted = {k: once(f"rooted_{k}") for k in ("var1", "var2", "ms1", "ms2")}
        normed = {k: once(f"normed_{k}") for k in ("var1", "var2")}
        xn2_ready, flat_ready = once("xn2"), once("flat_ready")
        kz_first, vl_first, va_first = once("kz_first"), once("vl_first"), once("va_first")
        pl_masked = [once(f"pl_masked{b}") for b in range(2)]
        pl_used = [once(f"pl_used{b}") for b in range(2)]
        dve_step, trig_step = once("dve_step"), once("trig_step")
        rot_ready, hid_by_pool = once("rot_ready"), once("hid_by_pool")
        q_parts, k_parts, qk_out = once("q_parts"), once("k_parts"), once("qk_out")
        stacks = [once(f"stack{n}") for n in range(SETS)]
        nm_ready, m_in = once("nm_ready"), once("m_in")
        p_used = once("p_used")
        rd_ready, yn_ready = once("rd_ready"), once("yn_ready")
        base_ready, xhi_ready, xlo_ready = once("base_ready"), once("xhi_ready"), once("xlo_ready")
        lge_ready, rw_ready, rw_out = once("lge_ready"), once("rw_ready"), once("rw_out")
        segments = [[] for _ in range(NM)]
        for e in range(NE):
            at = e * HID
            while at < (e + 1) * HID:
                end = min((e + 1) * HID, (at // 128 + 1) * 128)
                segments[at // 128].append((at % 128, at % 128 + end - at, e))
                at = end
        wb_in = [once(f"wb_in{m}") for m in range(NM)]
        gate_ready, hid_ready, hid_used = once("gate_ready"), once("hid_ready"), once("hid_used")
        stored = once("stored")
        phase_in, conv_in, norm_in, lin_in, attn_in, moe_in = (
            once(n) for n in ("phase_in", "conv_in", "norm_in", "lin_in", "attn_in", "moe_in"))
        x_loaded = [once(f"x_loaded{g}") for g in range(PAIRS)]
        pool_made, dve_made, wb_made = once("pool_made"), once("dve_made"), once("wb_made")
        wsplit, sines, conv_w = once("wsplit"), once("sines"), once("conv_w")

        block = ctx.enter_context(nc.Block())

        norm_consts = [(center[:], cen), (average[:], avg)]
        lin_consts = [(lin_ws[:], lin_w), (lin_b[:], lin_bqk), (lin_vb[:], lin_bv), (q_decay[:], qdec),
                      (k_decay[:], kdec), (keep01[:], mask01)]
        attn_consts = [(ln_ws[:], ln_w), (qkv_ws[:], qkv_w), (q_cos[:], qcos), (q_sin[:], qsin), (k_tab[:], ktab),
                       (ident[:], eye), (den_sel[:], dsel), (wo_ws[:], wo_w), (router_ws[:], router_w),
                       (rank_t[:], rank)]
        moe_consts = [(raw[0], w1T), (raw[1], w3T), (w2_ws[:].rearrange("p m c -> p (m c)"), w2T)]
        POOL_MADE, DVE_MADE = 23, 9

        def slot(step):
            return work[:, plan[step][0]:plan[step][0] + 1 + wide(step)]

        def wait_free(step):
            for before in plan[step][2]:
                wait_read(nc.tensor, before)

        def wait_full(eng, step):
            bank, use, _ = plan[step]
            eng.wait_ge(full[bank], use + 1)

        def wait_read(eng, step):
            bank, use, _ = plan[step]
            eng.wait_ge(free[bank], use + 1)

        def full_of(step):
            return full[plan[step][0]]

        def free_of(step):
            return free[plan[step][0]]

        def halves(tile):
            return tile[:, 0:T].rearrange("p (a t) -> p a t", a=2)

        def moe_index(g, c, m, b):
            return ((2 * g + c) * NM + m) * 2 + b

        MOE = [s for s in STEPS if s[0] == "moe"]

        def by_pool(n):
            return n % POOL_TAKES == POOL_TAKES - 1

        def wait_hidden(eng, n):
            if (n + 1) // POOL_TAKES:
                eng.wait_ge(hid_by_pool, (n + 1) // POOL_TAKES)
            eng.wait_ge(hid_ready, n + 1 - (n + 1) // POOL_TAKES)

        def load_routes(sp, g, c, m):
            for r0, r1, e in segments[m]:
                sp.dma_start(wb[r0:r1, m, :, :],
                             w_scr[g, :, e, c * HALF:(c + 1) * HALF].unsqueeze(0).broadcast_to([r1 - r0, 2, HALF]))\
                  .then_inc(wb_in[m], 16)

        @block.sync
        def _(sp):
            sp.dma_start(phase[:], ph).then_inc(phase_in, 16)
            sp.dma_start(pt[4][:, 0:8 * C], wr).then_inc(conv_in, 16)
            sp.dma_start(pt[5][:, 0:8 * C], wi).then_inc(conv_in, 16)
            for tile, src in norm_consts:
                sp.dma_start(tile, src).then_inc(norm_in, 16)
            for tile, src in lin_consts:
                sp.dma_start(tile, src).then_inc(lin_in, 16)
            for tile, src in attn_consts:
                sp.dma_start(tile, src).then_inc(attn_in, 16)
            sp.wait_ge(pool_made, POOL_MADE)

            def load_stacks(bt):
                g, b, n = bt // 2, bt % 2, bt % SETS
                for r in range(4):
                    rows = slice(16 * r, 16 * r + 16)
                    sp.dma_start(ks[n][rows].bitcast(f32), k_scr[g, r % 2, b].rearrange("h d t -> d h t"))\
                      .then_inc(stacks[n], 16)
                    sp.dma_start(qs[n][rows].bitcast(f32), q_scr[g, r // 2, b].rearrange("h d t -> d h t"))\
                      .then_inc(stacks[n], 16)
                sp.dma_start(qs[n][64:66].bitcast(f32), qs[n][66:68].bitcast(f32)).then_inc(stacks[n], 16)

            for step in STEPS:
                if step[0] == "v":
                    g = step[1]
                    for n in range(2):
                        sp.wait_ge(q_parts, 2 * g + n + 1)
                        sp.dma_start(q_scr[g, n].rearrange("b h d t -> (b h d) t"), parts[g][n][:].bitcast(f32))\
                          .then_inc(qk_out, 16)
                    for n in range(2):
                        sp.wait_ge(k_parts, 2 * g + n + 1)
                        sp.dma_start(k_scr[g, n].rearrange("b h d t -> (b h d) t"), kparts[n][:].bitcast(f32))\
                          .then_inc(qk_out, 16)
                    sp.wait_ge(qk_out, 64 * (g + 1))
                    for bt in ((0, 1) if g == 0 else (2,)):
                        load_stacks(bt)
                    if g:
                        for tile, src in moe_consts:
                            sp.dma_start(tile, src).then_inc(moe_in, 16)
                elif step[0] == "negmax":
                    bt = step[1]
                    wait_read(sp, step)
                    for hh in range(NH):
                        sp.dma_start(qs[bt % SETS][64:66, hh, :].bitcast(f32), nrow[2 * hh:2 * hh + 2, 0:T])\
                          .then_inc(m_in, 16)
                elif step[0] == "y" and step[1] + SETS < B:
                    wait_read(sp, ("score", step[1], NB - 1, NH - 1))
                    load_stacks(step[1] + SETS)
                elif step[0] == "rwT":
                    g = step[1]
                    wait_read(sp, step)
                    sp.dma_start(w_scr[g].rearrange("b e t -> (b e) t"), r_wT[:, 0:T]).then_inc(rw_out, 16)
                    if g == 0:
                        sp.wait_ge(rw_out, 16)
                        for m in range(NM):
                            load_routes(sp, 0, 0, m)
                elif step[0] == "moe" and step[4] == 1:
                    g, c, m = step[1:4]
                    ahead = 2 * g + c + 1
                    if ahead < 2 * PAIRS:
                        if ahead == 2 and m == 0:
                            sp.wait_ge(rw_out, 32)
                        wait_hidden(sp, moe_index(g, c, m, 1))
                        load_routes(sp, ahead // 2, ahead % 2, m)
                elif step[0] == "outT":
                    g = step[1]
                    wait_read(sp, step)
                    for b in range(2):
                        o = o_t[g].rearrange("p i (b c) -> p i b c", b=2)
                        sp.dma_start(out[2 * g + b, 0:640, :].rearrange("(i q) c -> q i c", q=128), o[:, 0:5, b, :])\
                          .then_inc(stored, 16)
                        sp.dma_start(out[2 * g + b, 640:TV, :], o[0:TV - 640, 5, b, :]).then_inc(stored, 16)
            sp.wait_ge(stored, 64 * PAIRS)

        @block.gpsimd
        def _(pool):
            for tile in (eye_b, neg_qk, neg_kq):
                nc.gpsimd.memset(tile[:], 0.0).then_inc(pool_made, 1)
            for bt in range(B):
                nc.gpsimd.memset(v_aug[bt][:], 0.0).then_inc(pool_made, 1)
            for n in range(SETS):
                nc.gpsimd.memset(qs[n].bitcast(f32), 0.0).then_inc(pool_made, 1)
                nc.gpsimd.memset(ks[n].bitcast(f32), 0.0).then_inc(pool_made, 1)
            pool.wait_ge(pool_made, 13)
            nc.gpsimd.affine_select(out=eye_b[:], in_=eye_b[:], compare_op=ALU.not_equal, fill=1.0, base=0,
                                    pattern=[[-1, 128]], channel_multiplier=1).then_inc(pool_made, 1)
            nc.gpsimd.affine_select(out=neg_qk[:], in_=neg_qk[:], compare_op=ALU.is_ge, fill=NEG, base=0,
                                    pattern=[[-1, 128]], channel_multiplier=1).then_inc(pool_made, 1)
            nc.gpsimd.affine_select(out=neg_kq[:], in_=neg_kq[:], compare_op=ALU.is_ge, fill=NEG, base=0,
                                    pattern=[[1, 128]], channel_multiplier=-1).then_inc(pool_made, 1)
            for n in range(SETS):
                pool.wait_ge(pool_made, 16 + n)
                nc.gpsimd.memset(ks[n][64:66].bitcast(f32), 1.0).then_inc(pool_made, 1)
            pool.wait_ge(pool_made, 16 + SETS)
            for bt in range(B):
                nc.gpsimd.memset(v_aug[bt][:, :, :, HD:HD + 1], 1.0).then_inc(pool_made, 1)
            pool.wait_ge(lin_in, 16 * len(lin_consts))
            for step in STEPS:
                if step[0] == "lin":
                    _, g, j, b = step
                    wait_read(pool, step)
                    part = p_lin[b][0:ROWS[j], 0:ROWS[j]]
                    nc.gpsimd.tensor_tensor(part, part, keep01[0:ROWS[j], 0:ROWS[j]], ALU.mult).then_inc(pl_masked[b], 1)
                elif step == ("qperm", 1):
                    wait_read(pool, ("q", 1))
                    wait_read(pool, step)
                    nc.gpsimd.tensor_tensor(rot[1], tmp1[1], tmp2[1], ALU.add).then_inc(rot_ready, 1)
                    pool.wait_ge(rot_ready, 1)
                    nc.gpsimd.tensor_copy(parts[1][0][:], rot[1]).then_inc(q_parts, 1)
                    pool.wait_ge(q_parts, 3)
                    nc.gpsimd.tensor_tensor(parts[1][1][:], rot[1], parts[1][0][:].bitcast(f32), ALU.subtract)\
                        .then_inc(q_parts, 1)
                elif step == ("k", 1):
                    wait_read(pool, step)
                    nc.gpsimd.tensor_tensor(krot[1], kza[1][0:64], kzb[1][0:64], ALU.add).then_inc(rot_ready, 1)
                    pool.wait_ge(rot_ready, 2)
                    pool.wait_ge(qk_out, 64)
                    nc.gpsimd.tensor_copy(kparts[0][:], krot[1]).then_inc(k_parts, 1)
                    pool.wait_ge(k_parts, 3)
                    nc.gpsimd.tensor_tensor(kparts[1][:], krot[1], kparts[0][:].bitcast(f32), ALU.subtract)\
                        .then_inc(k_parts, 1)
                elif step[0] == "split":
                    n = step[1] % 2
                    if step[1] < 2:
                        if n == 0:
                            pool.wait_ge(moe_in, 16 * len(moe_consts))
                            wait_read(pool, ("score", SETS - 1, NB - 1, NH - 1))
                        nc.gpsimd.tensor_copy(w_hi[n], raw[n]).then_inc(wsplit, 1)
                    else:
                        pool.wait_ge(wsplit, n + 1)
                        nc.gpsimd.tensor_tensor(w_lo[n], raw[n], w_hi[n].bitcast(f32), ALU.subtract)\
                          .then_inc(wsplit, 1)
                elif step[0] == "moe" and by_pool(moe_index(*step[1:])):
                    _, g, c, m, b = step
                    n = moe_index(g, c, m, b)
                    wait_read(pool, step)
                    pool.wait_ge(wb_in[m], (2 * g + c + 1) * 16 * len(segments[m]))
                    nc.gpsimd.tensor_tensor(hid[n % len(hid)], hid[n % len(hid)], wb[:, m, b, :], ALU.mult)\
                        .then_inc(hid_by_pool, 1)
                elif step[0] == "ms2":
                    g = step[1]
                    for b in range(2):
                        wait_read(pool, ("wo", 2 * g + b))
                    nc.gpsimd.tensor_tensor(h2[g], h2[g], x2[g], ALU.add).then_inc(base_ready, 1)

        @block.scalar
        def _(act):
            for g in range(PAIRS):
                for r in range(2):
                    act.dma_start(x_in[g][64 * r:64 * r + 64], xT[2 * g:2 * g + 2, :, r:r + XW].rearrange("b c t -> c b t"))\
                       .then_inc(x_loaded[g], 16)
            nc.scalar.preload_act_table_set("silu_and_others")
            act.wait_ge(trig_step, TRIG_STEPS)
            nc.scalar.activation(trig[:], trig[:], ACT.Sin).then_inc(sines, 1)
            nc.scalar.preload_act_table_set("natural_log_exp_and_others")
            act.wait_ge(dve_made, DVE_MADE)
            act.wait_ge(pool_made, POOL_MADE)

            def square(src, dst, kind):
                nc.scalar.activation(dst[:, 0:T], src[:, 0:T], ACT.Square).then_inc(squared[kind], 1)

            def inverse_root(step, dst, which):
                wait_full(act, step)
                nc.scalar.activation(halves(dst), slot(step)[:, :, 0:HALF], ACT.Ln,
                                     bias=eps[:, which:which + 1]).then_inc(free_of(step), 1)
                wait_read(act, step)
                nc.scalar.activation(dst[:, 0:T], dst[:, 0:T], ACT.Exp, scale=-0.5).then_inc(rooted[step[0]], 1)

            silu_loaded = False
            for step in STEPS:
                kind = step[0]
                if silu_loaded and kind in ("den", "ms2", "router"):
                    nc.scalar.preload_act_table_set("natural_log_exp_and_others")
                    silu_loaded = False
                if kind == "conv":
                    wait_full(act, step)
                    _, g, a = step
                    nc.scalar.activation(halves(h[g])[:, a], slot(step)[:, 0, 0:HALF], ACT.Copy)\
                      .then_inc(free_of(step), 1)
                elif kind in ("cen1", "cen2"):
                    g = step[1]
                    wait_full(act, step)
                    nc.scalar.activation(halves(sq[g]), slot(step)[:, :, 0:HALF], ACT.Square)\
                      .then_inc(squared["var" + kind[-1]], 1)
                    nc.scalar.activation(halves(cent[g]), slot(step)[:, :, 0:HALF], ACT.Copy)\
                      .then_inc(free_of(step), 1)
                elif kind in ("var1", "var2"):
                    inverse_root(step, rs[step[1]], 0)
                elif kind == "ms1":
                    g = step[1]
                    act.wait_ge(normed["var2"], g + 1)
                    square(x2[g], sq[g], kind)
                    inverse_root(step, rs[g], 1)
                elif kind == "lin":
                    _, g, j, b = step
                    wait_full(act, step)
                    if g * NB + j:
                        act.wait_ge(pl_used[b], g * NB + j)
                    cut = pieces(WIDTH[j])
                    w = cut[0][1]
                    nc.scalar.activation(
                        p_lin[b][0:ROWS[j], 0:WIDTH[j]].rearrange("p (a t) -> p a t", t=w),
                        slot(step)[0:ROWS[j], 0:len(cut), 0:w], ACT.Copy).then_inc(free_of(step), 1)
                elif kind == "v":
                    g = step[1]
                    wait_full(act, step)
                    vals = slot(step)[:, 0, 0:NB * 64].rearrange("p (i b h d) -> p i b h d", i=NB, b=2, h=NKV)
                    for b in range(2):
                        for i0, i1, m in ((0, NB - 1, 128), (NB - 1, NB, ROWS[-1])):
                            last = nc.scalar.activation(v_aug[2 * g + b][0:m, i0:i1, :, 0:HD], vals[0:m, i0:i1, b],
                                                        ACT.Copy)
                            last.then_inc(free_of(step) if (b, i0) == (1, NB - 1) else va_first, 1)
                elif kind == "negmax":
                    wait_full(act, step)
                    if step[1]:
                        act.wait_ge(m_in, 64 * step[1])
                    nc.scalar.activation(nrow.rearrange("p (a t) -> p a t", a=2), slot(step)[0:2 * NH, :, 0:384],
                                         ACT.Copy).then_inc(free_of(step), 1)
                elif kind == "score":
                    _, bt, j, hh = step
                    n = (bt * NB + j) * NH + hh
                    wait_full(act, step)
                    if n >= PT:
                        act.wait_ge(p_used, (n - PT) // NH + 1)
                    cut = pieces(WIDTH[j])
                    w = cut[0][1]
                    nc.scalar.activation(
                        pt[n % PT][0:ROWS[j], 0:WIDTH[j]].rearrange("p (a t) -> p a t", t=w),
                        slot(step)[0:ROWS[j], 0:len(cut), 0:w], ACT.Exp).then_inc(free_of(step), 1)
                elif kind == "y":
                    bt = step[1]
                    act.wait_ge(p_used, NB * (bt + 1))
                    if bt:
                        act.wait_ge(yn_ready, bt)
                    nc.scalar.activation(halves(ysb), acc[:, :, 0:HALF], ACT.Copy).then_inc(acc_out, 1)
                elif kind == "den":
                    wait_full(act, step)
                    nc.scalar.activation(halves(rden), slot(step)[:, :, 0:HALF], ACT.Ln).then_inc(free_of(step), 1)
                    wait_read(act, step)
                    nc.scalar.activation(rden, rden, ACT.Exp, scale=-1.0).then_inc(rd_ready, 1)
                elif kind == "ms2":
                    g = step[1]
                    for b in range(2):
                        wait_read(act, ("wo", 2 * g + b))
                    if g:
                        act.wait_ge(flat_ready, g)
                    square(x2[g], rs2, kind)
                    inverse_root(step, rs2, 1)
                elif kind == "router":
                    g = step[1]
                    act.wait_ge(flat_ready, g + 1)
                    for b in range(2):
                        rows = slice(64 * b, 64 * b + 64)
                        nc.scalar.activation(xs[g][b][rows], flat[rows, 0:T], ACT.Copy).then_inc(xhi_ready, 1)
                    wait_read(act, step)
                    nc.scalar.activation(ta[:], lg[:], ACT.Exp).then_inc(lge_ready, 1)
                elif kind == "rwT":
                    wait_full(act, step)
                    if step[1]:
                        act.wait_ge(rw_out, 16 * step[1])
                    nc.scalar.activation(r_wT.rearrange("p (a t) -> p a t", a=2), slot(step)[0:2 * NE, :, 0:384],
                                         ACT.Copy).then_inc(free_of(step), 1)
                elif kind == "moe":
                    n = moe_index(*step[1:])
                    silu_loaded = True
                    wait_full(act, step)
                    if n >= 4:
                        wait_read(act, MOE[n - 4])
                    nc.scalar.activation(gate[n % 4], slot(step)[:, 0, 0:HALF], ACT.Silu).then_inc(gate_ready, 1)
                elif kind == "outT":
                    g = step[1]
                    wait_full(act, step)
                    nc.scalar.activation(o_t[g].rearrange("p (a i) c -> p a (i c)", a=2),
                                         slot(step)[:, :, 0:384], ACT.Copy).then_inc(free_of(step), 1)

        @block.vector
        def _(v):
            v.wait_ge(phase_in, 16)
            steps = [0]

            def trig_link(ins):
                steps[0] += 1
                ins.then_inc(trig_step, 1)
                v.wait_ge(trig_step, steps[0])

            trig_link(nc.vector.tensor_scalar(trig[:, 0, :], phase[:], float(np.pi / 2), None, ALU.add))
            trig_link(nc.vector.tensor_copy(trig[:, 1, :], phase[:]))
            trig_link(nc.vector.tensor_scalar(turns[:], trig[:], float(1 / (2 * np.pi)), ROUND, ALU.mult, ALU.add))
            trig_link(nc.vector.tensor_scalar(turns[:], turns[:], ROUND, None, ALU.subtract))
            trig_link(nc.vector.scalar_tensor_tensor(out=trig[:], in0=turns[:], scalar=-6.28125, in1=trig[:],
                                                     op0=ALU.mult, op1=ALU.add))
            trig_link(nc.vector.scalar_tensor_tensor(out=trig[:], in0=turns[:], scalar=-(2 * np.pi - 6.28125),
                                                     in1=trig[:], op0=ALU.mult, op1=ALU.add))
            trig_link(nc.vector.tensor_scalar(trig[:], trig[:], 3.1415925, -3.1415925, ALU.min, ALU.max))
            assert steps[0] == TRIG_STEPS
            v.wait_ge(conv_in, 32)
            v.wait_ge(sines, 1)
            for tile, n in ((w_real, 0), (w_imag, 1)):
                nc.vector.tensor_tensor(tile, tile, trig[:, n, :].unsqueeze(2).broadcast_to([128, 8, C]),
                                        ALU.mult).then_inc(conv_w, 1)
            v.wait_ge(conv_w, 2)
            nc.vector.tensor_tensor(w_conv, w_real, w_imag, ALU.subtract).then_inc(conv_w, 1)
            nc.vector.memset(kz[0][0], 0.0).then_inc(dve_made, 1)
            nc.vector.memset(kz[0][1], 0.0).then_inc(dve_made, 1)
            nc.vector.memset(kz[1][0], 0.0).then_inc(dve_made, 1)
            nc.vector.memset(kz[1][1], 0.0).then_inc(dve_made, 1)
            for tile in h:
                nc.vector.memset(tile[:, T:TP], 0.0).then_inc(dve_made, 1)
            nc.vector.memset(smax[:], 0.0).then_inc(dve_made, 1)
            nc.vector.memset(eps[:, 0:1], 1e-5).then_inc(dve_made, 1)
            nc.vector.memset(eps[:, 1:2], 1e-6).then_inc(dve_made, 1)
            chain = [0]

            def link(ins):
                chain[0] += 1
                ins.then_inc(dve_step, 1)
                v.wait_ge(dve_step, chain[0])

            def add(ins):
                chain[0] += 1
                ins.then_inc(dve_step, 1)

            def over_experts(stat):
                return stat[:].unsqueeze(2).broadcast_to([128, 2 * NB, NE])

            def weigh(n):
                _, g, c, m, b = MOE[n]
                if by_pool(n):
                    return
                wait_read(v, MOE[n])
                if not b:
                    v.wait_ge(wb_in[m], (2 * g + c + 1) * 16 * len(segments[m]))
                nc.vector.tensor_tensor(hid[n % len(hid)], hid[n % len(hid)], wb[:, m, b, :], ALU.mult).then_inc(hid_ready, 1)

            for step in STEPS:
                kind, g = step[0], step[1] if len(step) > 1 else None
                if kind in ("var1", "var2"):
                    wait_read(v, ("cen" + kind[-1], g))
                    v.wait_ge(rooted[kind], g + 1)
                    nc.vector.tensor_tensor((xn if kind == "var1" else x2)[g], cent[g], rs[g], ALU.mult)\
                      .then_inc(normed[kind], 1)
                    if kind == "var2" and g == 0:
                        v.wait_ge(attn_in, 16 * len(attn_consts))
                    if kind == "var1" and g == 0:
                        v.wait_ge(lin_in, 16 * len(lin_consts))
                elif kind == "linq":
                    wait_full(v, step)
                    nc.vector.scalar_tensor_tensor(
                        out=halves(tmp1[g]), in0=slot(step)[:, :, 0:HALF], scalar=lin_b[:, 0:1],
                        in1=halves(q_decay), op0=ALU.add, op1=ALU.mult).then_inc(free_of(step), 1)
                elif kind == "link":
                    wait_full(v, step)
                    for b in range(2):
                        rows = slice(64 * b, 64 * b + 64)
                        nc.vector.scalar_tensor_tensor(
                            out=halves(kz[g][b])[rows], in0=slot(step)[rows, :, 0:HALF], scalar=lin_b[rows, 1:2],
                            in1=halves(k_decay)[rows], op0=ALU.add, op1=ALU.mult)\
                          .then_inc(free_of(step) if b else kz_first, 1)
                elif kind == "linv":
                    wait_full(v, step)
                    for i0, i1, m in ((0, 3, 128), (3, 5, 128), (5, 6, ROWS[-1])):
                        a = i0 // 3
                        nc.vector.tensor_tensor(
                            v_lin[g][0:m, i0:i1, :],
                            slot(step)[0:m, a, 128 * (i0 - 3 * a):128 * (i1 - 3 * a)].rearrange(
                                "p (i c) -> p i c", i=i1 - i0),
                            lin_vb[0:m].unsqueeze(1).broadcast_to([m, i1 - i0, 128]), ALU.add)\
                          .then_inc(free_of(step) if i0 == 5 else vl_first, 1)
                elif kind == "h2":
                    for b in range(2):
                        v.wait_ge(pl_used[b], NB * (g + 1))
                    nc.vector.tensor_tensor(halves(h2[g]), acc[:, :, 0:HALF], halves(h[g]), ALU.add).then_inc(acc_out, 1)
                elif kind == "ms1":
                    v.wait_ge(rooted[kind], g + 1)
                    nc.vector.scalar_tensor_tensor(out=xn[g], in0=x2[g], scalar=ln_ws[:, 0:1], in1=rs[g],
                                                   op0=ALU.mult, op1=ALU.mult).then_inc(xn2_ready, 1)
                elif kind == "q":
                    wait_full(v, step)
                    nc.vector.tensor_tensor(halves(tmp1[g]), slot(step)[:, :, 0:HALF], halves(q_cos), ALU.mult)\
                      .then_inc(free_of(step), 1)
                elif kind == "qperm":
                    wait_full(v, step)
                    nc.vector.tensor_tensor(halves(tmp2[g]), slot(step)[:, :, 0:HALF], halves(q_sin), ALU.mult)\
                      .then_inc(free_of(step), 1)
                    if g == 0:
                        wait_read(v, step)
                        link(nc.vector.tensor_tensor(rot[g], tmp1[g], tmp2[g], ALU.add))
                        nc.vector.tensor_copy(parts[g][0][:], rot[g]).then_inc(q_parts, 1)
                        v.wait_ge(q_parts, 1)
                        nc.vector.tensor_tensor(parts[g][1][:], rot[g], parts[g][0][:].bitcast(f32), ALU.subtract)\
                          .then_inc(q_parts, 1)
                elif kind == "k":
                    wait_full(v, step)
                    link(nc.vector.tensor_tensor(halves(kza[g])[0:64], slot(step)[0:64, :, 0:HALF],
                                                 halves(k_tab)[0:64], ALU.mult))
                    nc.vector.tensor_tensor(halves(kzb[g])[0:64], slot(step)[64:128, :, 0:HALF],
                                            halves(k_tab)[64:128], ALU.mult).then_inc(free_of(step), 1)
                    if g == 0:
                        wait_read(v, step)
                        link(nc.vector.tensor_tensor(krot[g], kza[g][0:64], kzb[g][0:64], ALU.add))
                        nc.vector.tensor_copy(kparts[0][:], krot[g]).then_inc(k_parts, 1)
                        v.wait_ge(k_parts, 1)
                        nc.vector.tensor_tensor(kparts[1][:], krot[g], kparts[0][:].bitcast(f32), ALU.subtract)\
                          .then_inc(k_parts, 1)
                elif kind == "v" and g == 1:
                    wait_full(v, step)
                    nc.vector.memset(wb_space[:, NM - 1, :], 0.0).then_inc(wb_made, 1)
                elif kind == "max":
                    i, w, heads = ROUNDS[step[2]]
                    m = ROWS[i]
                    wait_full(v, step)
                    to = smax[0:m, i, heads[0]:heads[-1] + 1]
                    if w > 512:
                        src, axis = slot(step)[0:m, 0:2, 0:w // 2], AX.XY
                    elif w == 128:
                        src, axis = slot(step)[0:m, 0, 0:NH * w].rearrange("p (g s) -> p g s", g=NH), AX.X
                    elif w == 256:
                        src, axis = slot(step)[0:m].rearrange("p a (g s) -> p (a g) s", g=2), AX.X
                    else:
                        src, axis = slot(step)[0:m, 0:2, 0:w], AX.X
                    nc.vector.tensor_reduce(to, src, axis, ALU.max).then_inc(free_of(step), 1)
                elif kind == "negmax":
                    bt = step[1]
                    wait_read(v, ("max", bt, len(ROUNDS) - 1))
                    if bt:
                        wait_full(v, ("negmax", bt - 1))
                    link(nc.vector.tensor_scalar(nmh[:], smax[:], -1.0, None, ALU.mult))
                    nc.vector.tensor_copy(nmx[:, :, :, 0], nmh[:].bitcast(f32)).then_inc(nm_ready, 1)
                    nc.vector.scalar_tensor_tensor(out=nmx[:, :, :, 1], in0=smax[:], scalar=-1.0,
                                                   in1=nmh[:].bitcast(f32), op0=ALU.mult, op1=ALU.subtract)\
                      .then_inc(nm_ready, 1)
                elif kind == "wo":
                    bt = step[1]
                    rows, res = slice(64 * (bt % 2), 64 * (bt % 2) + 64), halves(x2[bt // 2])
                    v.wait_ge(rd_ready, bt + 1)
                    nc.vector.tensor_tensor(yn, ysb, rden, ALU.mult).then_inc(yn_ready, 1)
                    wait_full(v, step)
                    nc.vector.tensor_tensor(res[rows], slot(step)[rows, :, 0:HALF], res[rows], ALU.add)\
                      .then_inc(free_of(step), 1)
                elif kind == "ms2":
                    if g:
                        v.wait_ge(xhi_ready, 2 * g)
                    v.wait_ge(rooted[kind], g + 1)
                    nc.vector.scalar_tensor_tensor(out=flat[:, 0:T], in0=x2[g], scalar=ln_ws[:, 1:2], in1=rs2,
                                                   op0=ALU.mult, op1=ALU.mult).then_inc(flat_ready, 1)
                elif kind == "router":
                    logits = slot(step)[:, 0, 0:2 * NB * NE].rearrange("p (g e) -> p g e", e=NE)
                    wait_full(v, step)
                    link(nc.vector.tensor_reduce(s1[:], logits, AX.X, ALU.max))
                    nc.vector.tensor_tensor(lg[:], logits, over_experts(s1), ALU.subtract).then_inc(free_of(step), 1)
                elif kind == "xlo":
                    b = step[2]
                    rows, other = slice(64 * b, 64 * b + 64), slice(64 - 64 * b, 128 - 64 * b)
                    v.wait_ge(xhi_ready, 2 * g + b + 1)
                    nc.vector.tensor_tensor(xs[g][b][other], flat[rows, 0:T], xs[g][b][rows].bitcast(f32),
                                            ALU.subtract).then_inc(xlo_ready, 1)
                elif kind == "top":
                    v.wait_ge(dve_step, chain[0])
                    k = step[2]
                    ranks = rank_t[:].unsqueeze(1).broadcast_to([128, 2 * NB, NE])
                    if k == 0:
                        v.wait_ge(lge_ready, g + 1)
                        link(nc.vector.tensor_reduce(s1[:], ta[:], AX.X, ALU.add))
                        add(nc.vector.reciprocal(s2[:], s1[:]))
                    elif k == 1:
                        link(nc.vector.tensor_tensor(lg[:], ta[:], over_experts(s2), ALU.mult))
                        add(nc.vector.tensor_reduce(s1[:], lg[:], AX.X, ALU.max))
                    elif k in (2, 6):
                        src, top = (lg, s1) if k == 2 else (ta, s2)
                        link(nc.vector.tensor_tensor(tb[:], src[:], over_experts(top), ALU.is_equal))
                        add(nc.vector.tensor_tensor(tb[:], tb[:], ranks, ALU.mult))
                    elif k in (3, 7):
                        link(nc.vector.tensor_reduce(s3[:], tb[:], AX.X, ALU.max))
                        add(nc.vector.tensor_tensor((oh if k == 3 else tb)[:], tb[:], over_experts(s3), ALU.is_equal))
                    elif k == 4:
                        add(nc.vector.scalar_tensor_tensor(out=ta[:], in0=oh[:], scalar=-2.0, in1=lg[:],
                                                           op0=ALU.mult, op1=ALU.add))
                    elif k == 5:
                        add(nc.vector.tensor_reduce(s2[:], ta[:], AX.X, ALU.max))
                    elif k == 8:
                        link(nc.vector.tensor_tensor(oh[:], oh[:], tb[:], ALU.add))
                        add(nc.vector.tensor_tensor(oh[:], oh[:], lg[:], ALU.mult))
                    elif k == 9:
                        link(nc.vector.scalar_tensor_tensor(out=s1[:], in0=s1[:], scalar=1e-9, in1=s2[:],
                                                            op0=ALU.add, op1=ALU.add))
                        add(nc.vector.reciprocal(s3[:], s1[:]))
                    elif k == 10:
                        nc.vector.tensor_tensor(ta[:], oh[:], over_experts(s3), ALU.mult).then_inc(rw_ready, 1)
                elif kind == "moe":
                    n = moe_index(*step[1:])
                    v.wait_ge(gate_ready, n + 1)
                    if n >= len(hid):
                        v.wait_ge(hid_used, (n - len(hid)) // 2 + 1)
                    nc.vector.tensor_tensor(hid[n % len(hid)], slot(step)[:, 1, 0:HALF], gate[n % 4], ALU.mult)\
                      .then_inc(free_of(step), 1)
                    if n:
                        weigh(n - 1)
                elif kind == "last":
                    weigh(len(MOE) - 1)
                elif kind == "fin":
                    _, g, c = step
                    v.wait_ge(base_ready, g + 1)
                    v.wait_ge(hid_used, (2 * g + c + 1) * NM)
                    nc.vector.tensor_tensor(halves(fin[g])[:, c], acc[:, c, 0:HALF], halves(h2[g])[:, c], ALU.add)\
                      .then_inc(acc_out, 1)

        @block.tensor
        def _(pe):
            pe.wait_ge(conv_w, 3)

            def mix(step, weights, src):
                wait_free(step)
                for a in range(2):
                    last = nc.tensor.matmul(slot(step)[:, a, 0:HALF], weights, halves(src)[:, a],
                                            start=True, stop=True)
                last.then_inc(full_of(step), 1)

            def down(n):
                g, c, m = MOE[2 * n][1:4]
                wait_hidden(pe, 2 * n + 1)
                for b in range(2):
                    last = nc.tensor.matmul(acc[64 * b:64 * b + 64, c, 0:HALF], w2_ws[:, m, :],
                                            hid[(2 * n + b) % len(hid)], start=(m == 0), stop=(m == NM - 1))
                last.then_inc(hid_used, 1)

            for step in STEPS:
                kind, g = step[0], step[1] if len(step) > 1 else None
                if kind == "conv":
                    wait_free(step)
                    pe.wait_ge(x_loaded[g], 32)
                    a = step[2]
                    for j in range(TAPS // 2):
                        for b in range(2):
                            last = nc.tensor.matmul(slot(step)[64 * b:64 * b + 64, 0, 0:HALF], w_conv[:, j, :],
                                                    x_in[g][:, b, 2 * j + HALF * a:2 * j + HALF * (a + 1)],
                                                    start=(j == 0), stop=(j == TAPS // 2 - 1))
                    last.then_inc(full_of(step), 1)
                elif kind == "cen1":
                    if g == 0:
                        pe.wait_ge(norm_in, 32)
                    wait_read(pe, ("conv", g, 0))
                    wait_read(pe, ("conv", g, 1))
                    mix(step, center[:], h[g])
                elif kind == "cen2":
                    pe.wait_ge(acc_out, ACC_OUT["h2", g])
                    mix(step, center[:], h2[g])
                elif kind in ("var1", "var2", "ms1", "ms2"):
                    pe.wait_ge(squared[kind], g + 1)
                    mix(step, average[:], rs2 if kind == "ms2" else sq[g])
                elif kind in ("linq", "link"):
                    if kind == "linq":
                        if g == 0:
                            pe.wait_ge(lin_in, 16 * len(lin_consts))
                        pe.wait_ge(normed["var1"], g + 1)
                    mix(step, lin_ws[:, 0 if kind == "linq" else 1, :], xn[g])
                elif kind == "linv":
                    wait_free(step)
                    for i in range(NB):
                        last = nc.tensor.matmul(slot(step)[0:ROWS[i], i // 3, 128 * (i % 3):128 * (i % 3) + 128],
                                                xn[g][:, 128 * i:128 * i + ROWS[i]], lin_ws[:, 2, :],
                                                start=True, stop=True)
                    last.then_inc(full_of(step), 1)
                elif kind == "lin":
                    _, g, j, b = step
                    if j == 0 and b == 0:
                        wait_read(pe, ("linq", g))
                        pe.wait_ge(kz_first, g + 1)
                        wait_read(pe, ("link", g))
                    wait_free(step)
                    for n, (o, w) in enumerate(pieces(WIDTH[j])):
                        last = nc.tensor.matmul(slot(step)[0:ROWS[j], n, 0:w], kz[g][b][:, 128 * j:128 * j + ROWS[j]],
                                                tmp1[g][:, 128 * j + o:128 * j + o + w], start=True, stop=True)
                    last.then_inc(full_of(step), 1)
                elif kind == "lv":
                    j = step[2]
                    if j == 0:
                        pe.wait_ge(vl_first, 2 * g + 2)
                        wait_read(pe, ("linv", g))
                        if g:
                            pe.wait_ge(acc_out, ACC_OUT["h2", g - 1])
                    for b in range(2):
                        pe.wait_ge(pl_masked[b], g * NB + j + 1)
                        for a, t0, t1 in spans(j):
                            last = nc.tensor.matmul(acc[64 * b:64 * b + 64, a, t0 - a * HALF:t1 - a * HALF],
                                                    v_lin[g][0:ROWS[j], j, 64 * b:64 * b + 64],
                                                    p_lin[b][0:ROWS[j], t0 - 128 * j:t1 - 128 * j],
                                                    start=(j == 0), stop=(j == NB - 1 or (a == 0 and j == 2)))
                        last.then_inc(pl_used[b], 1)
                elif kind in ("q", "qperm", "k"):
                    if kind == "q":
                        if g == 0:
                            pe.wait_ge(attn_in, 16 * len(attn_consts))
                        pe.wait_ge(xn2_ready, g + 1)
                    n = ("q", "qperm", "k").index(kind)
                    mix(step, qkv_ws[:, 128 * n:128 * n + 128], xn[g])
                elif kind == "v":
                    wait_free(step)
                    for i in range(NB):
                        last = nc.tensor.matmul(slot(step)[0:ROWS[i], 0, 64 * i:64 * i + 64],
                                                xn[g][:, 128 * i:128 * i + ROWS[i]], qkv_ws[:, 384:448],
                                                start=True, stop=True)
                    last.then_inc(full_of(step), 1)
                elif kind == "max":
                    bt = step[1]
                    i, w, heads = ROUNDS[step[2]]
                    b, m, cut = bt % SETS, ROWS[i], pieces(w)
                    if step[2] == 0:
                        pe.wait_ge(stacks[b], 144 * (bt // SETS + 1))
                        if bt == 0:
                            pe.wait_ge(pool_made, POOL_MADE)
                    wait_free(step)
                    for n, hh in enumerate(heads):
                        for k, (o, cw) in enumerate(cut):
                            bank, col = n + k, 0
                            if w == 128:
                                bank, col = 0, n * w
                            elif w == 256:
                                bank, col = n // 2, n % 2 * w
                            diag = k == len(cut) - 1
                            nc.tensor.matmul(slot(step)[0:m, bank, col:col + cw],
                                             qs[b][:, hh, 128 * i:128 * i + m], ks[b][:, hh // 2, o:o + cw],
                                             start=True, stop=not diag)
                            if diag:
                                last = nc.tensor.matmul(slot(step)[0:m, bank, col + cw - m:col + cw],
                                                        eye_b[:, 0:m], neg_qk[:, 0:m], start=False, stop=True)
                    last.then_inc(full_of(step), 1)
                elif kind == "negmax":
                    pe.wait_ge(nm_ready, 2 * step[1] + 2)
                    wait_free(step)
                    for i in range(NB):
                        last = nc.tensor.matmul(slot(step)[0:2 * NH, i // 3, 128 * (i % 3):128 * (i % 3) + 128],
                                                nmx[0:ROWS[i], i].rearrange("p h n -> p (h n)"),
                                                ident[0:ROWS[i], :], start=True, stop=True)
                    last.then_inc(full_of(step), 1)
                elif kind == "score":
                    _, bt, j, hh = step
                    b = bt % SETS
                    if j == 0 and hh == 0:
                        pe.wait_ge(m_in, 64 * (bt + 1))
                    wait_free(step)
                    for n, (o, w) in enumerate(pieces(WIDTH[j])):
                        nc.tensor.matmul(slot(step)[0:ROWS[j], n, 0:w], ks[b][:, hh // 2, 128 * j:128 * j + ROWS[j]],
                                         qs[b][:, hh, 128 * j + o:128 * j + o + w], start=True, stop=(n > 0))
                    nc.tensor.matmul(slot(step)[0:ROWS[j], 0, 0:ROWS[j]], eye_b[:, 0:ROWS[j]],
                                     neg_kq[:, 0:ROWS[j]], start=False, stop=True).then_inc(full_of(step), 1)
                elif kind == "pv":
                    _, bt, j = step
                    if j == 0:
                        if bt % 2 == 0:
                            pe.wait_ge(va_first, 3 * (bt // 2 + 1))
                            wait_read(pe, ("v", bt // 2))
                        pe.wait_ge(acc_out, ACC_OUT["y", bt] - 1)
                    for hh in range(NH):
                        n = (bt * NB + j) * NH + hh
                        wait_read(pe, ("score", bt, j, hh))
                        for a, t0, t1 in spans(j):
                            last = nc.tensor.matmul(
                                acc[32 * hh:32 * hh + 32, a, t0 - a * HALF:t1 - a * HALF],
                                v_aug[bt][0:ROWS[j], j, hh // 2, :],
                                pt[n % PT][0:ROWS[j], t0 - 128 * j:t1 - 128 * j],
                                start=(j == 0), stop=(j == NB - 1 or (a == 0 and j == 2)))
                    last.then_inc(p_used, 1)
                elif kind == "den":
                    pe.wait_ge(acc_out, ACC_OUT["y", step[1]])
                    mix(step, den_sel[:], ysb)
                elif kind == "wo":
                    b = step[1] % 2
                    wait_free(step)
                    pe.wait_ge(yn_ready, step[1] + 1)
                    for a in range(2):
                        last = nc.tensor.matmul(slot(step)[64 * b:64 * b + 64, a, 0:HALF], wo_ws[:], halves(yn)[:, a],
                                                start=True, stop=True)
                    last.then_inc(full_of(step), 1)
                elif kind == "router":
                    pe.wait_ge(flat_ready, g + 1)
                    wait_free(step)
                    for i in range(NB):
                        last = nc.tensor.matmul(slot(step)[:, 0, 2 * NE * i:2 * NE * (i + 1)],
                                                flat[:, 128 * i:128 * i + 128], router_ws[:], start=True, stop=True)
                    last.then_inc(full_of(step), 1)
                elif kind == "rwT":
                    pe.wait_ge(rw_ready, g + 1)
                    wait_free(step)
                    for i in range(NB):
                        last = nc.tensor.matmul(slot(step)[0:2 * NE, i // 3, 128 * (i % 3):128 * (i % 3) + 128],
                                                ta[:, 2 * i:2 * i + 2, :].rearrange("p b e -> p (b e)"), ident[:],
                                                start=True, stop=True)
                    last.then_inc(full_of(step), 1)
                elif kind == "moe":
                    _, g, c, m, b = step
                    n = moe_index(g, c, m, b)
                    if (c, m, b) == (0, 0, 0):
                        pe.wait_ge(xhi_ready, 2 * g + 2)
                        pe.wait_ge(xlo_ready, 2 * g + 2)
                        if g == 0:
                            pe.wait_ge(wsplit, 4)
                    wait_free(step)
                    for k in range(2):
                        for part in (w_hi, w_lo):
                            last = nc.tensor.matmul(slot(step)[:, k, 0:HALF], part[k][:, 128 * m:128 * m + 128],
                                                    halves(xs[g][b])[:, c], start=(part is w_hi), stop=(part is w_lo))
                    last.then_inc(full_of(step), 1)
                    if b and n // 2 >= LAG:
                        lagged = n // 2 - LAG
                        if lagged % NM == 0:
                            before = ACC_OUT["y", B - 1] if lagged < 2 * NM else ACC_OUT["fin", 0, lagged // NM - 2]
                            pe.wait_ge(acc_out, before)
                        down(lagged)
                elif kind == "last":
                    for n in range(len(MOE) // 2 - LAG, len(MOE) // 2):
                        down(n)
                elif kind == "outT":
                    pe.wait_ge(acc_out, ACC_OUT["fin", g, 1])
                    wait_free(step)
                    for i in range(NB):
                        last = nc.tensor.transpose(slot(step)[:, i // 3, 128 * (i % 3):128 * (i % 3) + 128],
                                                   fin[g][:, 128 * i:128 * i + 128], ident[:])
                    last.then_inc(full_of(step), 1)


_OUT = (B, TV, C)


def _layouts(inputs):
    f = np.float32
    a = {k: np.asarray(v) for k, v in inputs.items()}

    def twice(w):
        z = np.zeros((2 * w.shape[0], 2 * w.shape[1]), f)
        z[:w.shape[0], :w.shape[1]] = w
        z[w.shape[0]:, w.shape[1]:] = w
        return z

    got = {}
    x = np.zeros((B, C, XW + 1), f)
    x[..., :S_IN] = a["x"].transpose(0, 2, 1)
    got["xT"] = x
    for name, key in (("wr", "L0_tok_w_real"), ("wi", "L0_tok_w_imag")):
        w = a[key].transpose(2, 1, 0).reshape(TAPS // 2, 2, C, C)
        got[name] = w.transpose(1, 2, 0, 3).reshape(128, -1)
    got["ph"] = np.repeat(a["L0_tok_phases"].reshape(TAPS // 2, 2).T, 64, axis=0)
    w, bias = a["L0_attn_Wqkv"], a["L0_attn_bqkv"]
    got["lin_w"] = np.stack([twice(w[:, 64 * n:64 * n + 64]) for n in range(3)], axis=1)
    got["lin_bqk"] = np.stack([np.tile(bias[64 * n:64 * n + 64], 2) for n in range(2)], axis=1)
    got["lin_bv"] = np.broadcast_to(np.tile(bias[128:192], 2), (128, 128))
    got["ln_w"] = np.stack([np.tile(a["L0_ffn_ln1_w"], 2), np.tile(a["L0_ffn_ln2_w"], 2)], axis=1)
    d = np.arange(64)
    partner = d // HD * HD + (d % HD + HD // 2) % HD
    wq, wk, wv = (a[f"L0_ffn_{n}"] for n in ("wq", "wk", "wv"))
    got["qkv_w"] = np.concatenate([twice(wq.T), twice(wq[partner].T), twice(wk.T), twice(wk[partner[:32]].T),
                                   twice(wv.T)], axis=1)
    wo = np.zeros((NH, 32, C), f)
    wo[:, :HD] = a["L0_ffn_wo"].T.reshape(NH, HD, C)
    got["wo_w"] = wo.reshape(128, C)
    got["router_w"] = twice(a["L0_ffn_router_w"].T)
    for name, key in (("w1T", "L0_ffn_w1"), ("w3T", "L0_ffn_w3")):
        w = np.zeros((2, C, MP), f)
        w[:, :, :NE * HID] = a[key].transpose(2, 0, 1).reshape(C, NE * HID)
        got[name] = w.reshape(128, MP)
    w = np.zeros((MP, C), f)
    w[:NE * HID] = a["L0_ffn_w2"].transpose(0, 2, 1).reshape(NE * HID, C)
    got["w2T"] = w.reshape(NM, 128, C).transpose(1, 0, 2).reshape(128, -1)
    got["eye"] = np.eye(128, dtype=f)
    got["cen"] = twice(np.eye(64, dtype=f) - f(1 / 64))
    got["avg"] = twice(np.full((64, 64), 1 / 64, f))
    sel = np.zeros((128, 128), f)
    for hh in range(NH):
        sel[32 * hh + HD, 32 * hh:32 * hh + 32] = 1
    got["dsel"] = sel
    t = np.arange(T)
    got["qdec"] = np.broadcast_to((ALPHA ** t / 8).astype(f), (128, T))
    got["kdec"] = np.broadcast_to((ALPHA ** -t.astype(np.float64)).astype(f), (128, T))
    inv = (1.0 / 10000.0 ** (np.arange(0, HD, 2, dtype=f) / HD)).astype(f)
    angle = np.outer(t.astype(f), inv).astype(f)
    cos = np.tile(np.cos(angle), (1, 2)).T.astype(f)
    sin = np.concatenate([-np.sin(angle), np.sin(angle)], axis=1).T.astype(f)
    got["qcos"] = np.tile(cos, (8, 1)) * f(HD ** -0.5)
    got["qsin"] = np.tile(sin, (8, 1)) * f(HD ** -0.5)
    got["ktab"] = np.concatenate([np.tile(cos, (4, 1)), np.tile(sin, (4, 1))])
    got["rank"] = np.broadcast_to(np.arange(NE, 0, -1).astype(f), (128, NE))
    got["mask01"] = np.triu(np.ones((128, 128), f))
    return {k: np.ascontiguousarray(v) for k, v in got.items()}


def kernel(**inputs):
    import concourse.bacc as bacc
    from concourse.bass_utils import run_bass_kernel_spmd

    nc = bacc.Bacc("TRN2", target_bir_lowering=False, num_devices=1)
    arrays = _layouts(inputs)
    args = {k: nc.dram_tensor(f"in_{k}", v.shape, mybir.dt.from_np(v.dtype), kind="ExternalInput").ap()
            for k, v in arrays.items()}
    out = nc.dram_tensor("out_layer", _OUT, mybir.dt.float32, kind="ExternalOutput").ap()
    audio_tower(nc, **args, out=out)
    r = run_bass_kernel_spmd(nc, [{f"in_{k}": v for k, v in arrays.items()}], core_ids=[0])
    return r.results[0]["out_layer"]
```

```python
from contextlib import ExitStack
from itertools import product

import numpy as np

import concourse.bass as bass
from concourse import mybir

B, S_IN, C, TAPS = 4, 750, 64, 16
TV = S_IN - TAPS + 1
T = TV + TV % 2
TP = 768
HALF = T // 2
PAIRS = B // 2
NB = (T + 127) // 128
WIDTH = [T - 128 * j for j in range(NB)]
ROWS = [min(128, w) for w in WIDTH]
NH, NKV, HD = 4, 2, 16
NE, HID = 8, int(8 / 3 * C)
NM = (NE * HID + 127) // 128
MP = NM * 128
XW = S_IN + 1
ALPHA = float(np.float32(0.99))
NEG = -1e30
BANKS = 6
TRIG_STEPS = 7
ROUND = 12582912.0
PT = 8
STACK = (0, 2, 1, 0)
SETS = max(STACK) + 1
TOP_STEPS = 11
POOL_TAKES = 2
CUTS = 4
IDLE_PRODUCTS = 15
LAG = 2


def pieces(width):
    return [(0, width)] if width <= 512 else [(0, width // 2), (width // 2, width // 2)]


def spans(j):
    return [(a, max(128 * j, a * HALF), (a + 1) * HALF) for a in range(2) if 128 * j < (a + 1) * HALF]


def score_rounds():
    out = []
    for i in range(NB):
        w = min(128 * (i + 1), T)
        n = max(1, 512 // w)
        out += [(i, w, tuple(range(h, h + n))) for h in range(0, NH, n)]
    return out


ROUNDS = score_rounds()


ORDER = """
conv 0 0-1, cen1 0, var1 0, conv 1 0, linq 0, conv 1 1, link 0, cen1 1, linv 0, lin 0 0 0 0-1, var1 1
lin 0 0 1 0-1, lin 0 1 0-1 0-1, lv 0 0, lin 0 2 0-1 0, lv 0 1, lin 0 3 0-1 0, lv 0 2, lin 0 4 0-1 0, lv 0 3
lin 0 5 0-1 0, linq 1, lv 0 4-5, h2 0, link 1, cen2 0, linv 1, var2 0, lin 1 0 0-1 0-1, ms1 0, lin 1 1 0-1 0-1
lv 1 0, q 0, qperm 0, lin 1 2 0-1 0, lv 1 1, k 0, lin 1 3 0-1 0, lv 1 2, lin 1 4 0-1 0, lv 1 3, lin 1 5 0-1 0
lv 1 4-5, h2 1, cen2 1, var2 1, v 0, max 0 0-11, ms1 1, max 0 12-14, q 1, max 0 15-17, qperm 1, max 0 18
negmax 0, max 1 0, k 1, max 1 1-2, v 1, score 0 0 0 0-1, max 1 3, score 0 0 1 0, max 1 4-6, score 0 0 1 1
max 1 7-9, score 0 0 2 0, max 1 10-11, score 0 0 2 1, max 1 12, score 0 0 3 0, max 1 13-14, score 0 0 3 1
score 0 1 0 0-1, score 0 1 1 0, pv 0 0, score 0 1 1 1, score 0 1 2 0, max 1 15, score 0 1 2 1, max 1 16
score 0 1 3 0-1, score 0 2 0-1 0, max 1 17-18, score 0 2 2 0, pv 0 1, negmax 1, score 0 2 3 0, max 2 0
score 0 3 0-1 0, max 2 1-2, pv 0 2, score 0 3 2 0, max 2 3-5, score 0 3 3 0, score 0 4 0-1 0, max 2 6
score 0 4 2 0, pv 0 3, max 2 7, score 0 4 3 0, score 0 5 0-2 0, max 2 8-9, pv 0 4, score 0 5 3 0, max 2 10
score 1 0 0 0-1, pv 0 5, max 2 11, score 1 0 1 0, max 2 12, y 0, score 1 0 1 1, score 1 0 2 0-1, max 2 13
score 1 0 3 0-1, max 2 14-15, den 0, max 2 16, score 1 1 0 0, pv 1 0, score 1 1 0 1, score 1 1 1 0-1, wo 0
score 1 1 2-3 0-1, score 1 2 0-1 0, max 2 17-18, pv 1 1, score 1 2 2 0, negmax 2, max 3 0, score 1 2 3 0
score 1 3 0 0, max 3 1, score 1 3 1-2 0, max 3 2-3, score 1 3 3 0, pv 1 2, score 1 4 0-1 0, max 3 4-5
score 1 4 2-3 0, pv 1 3, max 3 6-8, pv 1 4, score 1 5 0-1 0, max 3 9, score 1 5 2 0, max 3 10, score 1 5 3 0
score 2 0 0 0-1, split 0, pv 1 5, score 2 0 1 0, y 1, max 3 11, score 2 0 1 1, score 2 0 2 0, max 3 12
score 2 0 2 1, score 2 0 3 0, split 1, score 2 0 3 1, max 3 13, split 2, pv 2 0, score 2 1 0 0-1, score 2 1 1 0
den 1, score 2 1 1 1, split 3-4, score 2 1 2 0, max 3 14, score 2 1 2 1, score 2 1 3 0, wo 1, score 2 1 3 1
score 2 2 0 0, max 3 15, pv 2 1, score 2 2 1 0, max 3 16, score 2 2 2-3 0, score 2 3 0 0, split 5, score 2 3 1 0
max 3 17, score 2 3 2 0, max 3 18, pv 2 2, score 2 3 3 0, score 2 4 0 0, split 6, pv 2 3, score 2 4 1-3 0
negmax 3, pv 2 4, score 2 5 0 0, split 7, score 2 5 1-3 0, ms2 0, score 3 0 0 0, split 8, score 3 0 0 1, pv 2 5
score 3 0 1 0, y 2, score 3 0 1 1, score 3 0 2-3 0-1, den 2, split 9, router 0, split 10, score 3 1 0 0, pv 3 0
wo 2, split 11, score 3 1 0 1, score 3 1 1 0, top 0 0, score 3 1 1 1, score 3 1 2 0-1, score 3 1 3 0, top 0 1-2
score 3 1 3 1, score 3 2 0-2 0, split 12, score 3 2 3 0, pv 3 1, score 3 3 0 0, split 13, score 3 3 1-2 0
pv 3 2, score 3 3 3 0, top 0 3, split 14, top 0 4, score 3 4 0-1 0, top 0 5-7, score 3 4 2-3 0, pv 3 3
score 3 5 0-1 0, top 0 8, score 3 5 2 0, xlo 0 1, top 0 9, score 3 5 3 0, split 15, top 0 10, rwT 0, pv 3 4-5
xlo 0 0, y 3, moe 0 0 0 0-1, moe 0 0 1 0, den 3, wo 3, moe 0 0 1 1, moe 0 0 2 0-1, ms2 1, moe 0 0 3-4 0-1
router 1, top 1 0-1, moe 0 0 5 0-1, moe 0 0 6 0, top 1 2, moe 0 0 6 1, top 1 3, moe 0 0 7 0, top 1 4
moe 0 0 7 1, top 1 5, moe 0 0 8 0, top 1 6, moe 0 0 8 1, top 1 7, moe 0 0 9 0, top 1 8, moe 0 0 9 1, top 1 9
moe 0 0 10 0, top 1 10, moe 0 0 10 1, xlo 1 0, moe 0 1 0 0, rwT 1, moe 0 1 0 1, moe 0 1 1-2 0-1, fin 0 0
moe 0 1 3-4 0-1, xlo 1 1, moe 0 1 5-10 0-1, moe 1 0 0-4 0-1, fin 0 1, moe 1 0 5-10 0-1, outT 0, moe 1 1 0-1 0-1
moe 1 1 2 0, fin 1 0, moe 1 1 2 1, moe 1 1 3-10 0-1, last, fin 1 1, outT 1
"""


def schedule():
    out = []
    for entry in ORDER.replace("\n", ",").split(","):
        if entry:
            kind, *at = entry.split()
            ends = [[int(end) for end in n.split("-")] for n in at]
            out += [(kind, *n) for n in product(*(range(e[0], e[-1] + 1) for e in ends))]
    return out


BANKLESS = ("xlo", "top", "split", "lv", "h2", "pv", "y", "fin", "last")
STEPS = schedule()


def wide(step):
    if step[0] == "max":
        return ROUNDS[step[2]][1] > 512
    return step[0] not in ("conv", "lin", "v", "score", "router")


def bank_plan():
    plan, last, uses, at = {}, {}, [0] * BANKS, 0
    for step in STEPS:
        if step[0] not in BANKLESS:
            if wide(step):
                at += at % 2
            banks = [(at + n) % BANKS for n in range(1 + wide(step))]
            before = {last[bank] for bank in banks if bank in last}
            plan[step] = banks[0], uses[banks[0]], sorted(before, key=STEPS.index)
            uses[banks[0]] += 1
            for bank in banks:
                last[bank] = step
            at = (at + len(banks)) % BANKS
    return plan


def audio_tower(nc, xT, wr, wi, ph, lin_w, lin_bqk, lin_bv, ln_w, qkv_w, wo_w, router_w,
                w1T, w3T, w2T, eye, cen, avg, dsel, qdec, kdec, qcos, qsin, ktab, rank, out):
    f32, f32r, bf16 = mybir.dt.float32, mybir.dt.float32r, mybir.dt.bfloat16
    ALU, ACT, AX = mybir.AluOpType, mybir.ActivationFunctionType, mybir.AxisListType

    q_scr = nc.dram_tensor("q_scratch", [PAIRS, 2, 2, NH, HD, T], f32).ap()
    k_scr = nc.dram_tensor("k_scratch", [PAIRS, 2, 2, NKV, HD, T], f32).ap()
    w_scr = nc.dram_tensor("route_scratch", [PAIRS, 2, NE, T], f32).ap()

    with ExitStack() as ctx:
        def sb(name, shape, dt=f32):
            return ctx.enter_context(nc.sbuf_tensor(name, shape, dt))

        def once(name):
            return ctx.enter_context(nc.semaphore(name))

        phase = sb("phase", [128, 8])
        trig = sb("trig", [128, 2, 8])
        turns = sb("turns", [128, 2, 8])
        lin_ws = sb("lin_ws", [128, 3, 128])
        lin_b = sb("lin_b", [128, 2])
        lin_vb = sb("lin_vb", [128, 128])
        ln_ws = sb("ln_ws", [128, 2])
        qkv_ws = sb("qkv_ws", [128, 3 * 128 + 64])
        wo_ws = sb("wo_ws", [128, C])
        router_ws = sb("router_ws", [128, 2 * NE])
        w_split = sb("w_split", [128, 4 * MP], f32r)
        w_hi, w_lo = ([w_split[:, n * MP:(n + 1) * MP] for n in pair] for pair in ((0, 1), (2, 3)))
        w2_ws = sb("w2_ws", [128, NM, C])
        ident = sb("ident", [128, 128])
        center = sb("center", [128, 128])
        average = sb("average", [128, 128])
        den_sel = sb("den_sel", [128, 128])
        q_decay = sb("q_decay", [128, T])
        k_decay = sb("k_decay", [128, T])
        q_cos = sb("q_cos", [128, T])
        q_sin = sb("q_sin", [128, T])
        k_tab = sb("k_tab", [128, T])
        rank_t = sb("rank_t", [128, NE])
        eye_b = sb("eye_b", [128, 128], bf16)
        neg_qk = sb("neg_qk", [128, 128], bf16)
        eps = sb("eps", [128, 2])

        wb_space = sb("wb_space", [128, NM, T])
        wb = wb_space[:].rearrange("p m (b t) -> p m b t", b=2)

        first_space = sb("first_space", [128, 8, T])
        cent, tmp2, rs, xn, sq, tmp1, kza, kzb = ([space[:, n, :] for space in (first_space, wb_space)]
                                                  for n in range(8))
        kz = list(zip(kza, kzb))
        x_in = [space[:, n:n + 3, :].rearrange("p m t -> p (m t)")[:, 0:2 * XW].rearrange("p (b t) -> p b t", b=2)
                for space, n in ((first_space, 2), (wb_space, 8))]
        h = [sb(f"h{g}", [128, TP])[:] for g in range(PAIRS)]
        h2 = [sb(f"h2_{g}", [128, T])[:] for g in range(PAIRS)]
        x2 = [sb(f"x2_{g}", [128, T])[:] for g in range(PAIRS)]
        v_lin = [sb(f"v_lin{g}", [128, NB, 128])[:] for g in range(PAIRS)]
        parts = [[sb(f"part{g}{n}", [128, T], f32r) for n in range(2)] for g in range(PAIRS)]
        kparts = [sb(f"kpart{n}", [64, T], f32r) for n in range(2)]
        qs = [sb(f"qs{b}", [128, NH, T], f32r)[:] for b in range(2)]
        ks = [sb(f"ks{b}", [128, NKV, T], f32r)[:] for b in range(2)]
        qs.append(w_split[:, 0:NH * T].rearrange("p (h t) -> p h t", h=NH))
        ks.append(w_split[:, NH * T:(NH + NKV) * T].rearrange("p (h t) -> p h t", h=NKV))
        v_aug = [sb(f"v_aug{b}", [128, NB, NKV, 32]) for b in range(B)]
        smax = sb("smax", [128, NB, NH])
        nmx = sb("nmx", [128, NB, NH, 2])
        nmh = sb("nmh", [128, NB, NH], f32r)
        exps = sb("exps", [128, PT, T])
        pt = [exps[:, n, :] for n in range(PT)]
        lg, ta, tb, oh = (sb(n, [128, 2 * NB, NE]) for n in ("lg", "ta", "tb", "oh"))
        s1, s2, s3 = (sb(n, [128, 2 * NB]) for n in ("s1", "s2", "s3"))
        raw = [first_space[:, n:n + 2].rearrange("p a t -> p (a t)")[:, 0:MP] for n in (4, 6)]
        w_real, w_imag, w_conv = (pt[n][:, 0:8 * C].rearrange("p (j c) -> p j c", c=C) for n in (4, 5, 6))
        idle = pt[7][:, 0:256].bitcast(bf16)
        p_lin = pt[4:6]
        rot, krot, fin, xs, flat = sq, [tile[0:64] for tile in cent], h, parts, h[1]
        ysb, rden, yn, rs2 = cent[0], rs[0], xn[0], tmp2[0]
        nrow = v_lin[0].rearrange("p i c -> p (i c)")[0:2 * NH]
        r_wT = v_lin[1].rearrange("p i c -> p (i c)")[0:2 * NE]
        gate = [(q_cos, q_sin)[n // 2][:, n % 2 * HALF:(n % 2 + 1) * HALF] for n in range(4)]
        hid = [pt[n // 2][:, n % 2 * HALF:(n % 2 + 1) * HALF] for n in range(2 * (LAG + 1))]
        o_t = v_lin

        work = ctx.enter_context(nc.psum_tensor("work", [128, BANKS, 512], f32))
        acc = ctx.enter_context(nc.psum_tensor("acc", [128, 2, 512], f32))

        plan = bank_plan()
        full = [once(f"full{n}") for n in range(BANKS)]
        free = [once(f"free{n}") for n in range(BANKS)]
        ACC_OUT = {("h2", 0): 1, ("h2", 1): 2, **{("y", bt): 3 + bt for bt in range(B)},
                   **{("fin", g, c): 7 + 2 * g + c for g in range(PAIRS) for c in range(2)}}
        acc_out = once("acc_out")
        squared = {k: once(f"squared_{k}") for k in ("var1", "var2", "ms1", "ms2")}
        rooted = {k: once(f"rooted_{k}") for k in ("var1", "var2", "ms1", "ms2")}
        normed = {k: once(f"normed_{k}") for k in ("var1", "var2")}
        xn2_ready, flat_ready = once("xn2"), once("flat_ready")
        kz_first, vl_first, va_first = once("kz_first"), once("vl_first"), once("va_first")
        p_masked = once("p_masked")
        pl_masked = [once(f"pl_masked{b}") for b in range(2)]
        pl_used = [once(f"pl_used{b}") for b in range(2)]
        dve_step, trig_step = once("dve_step"), once("trig_step")
        rot_ready, hid_by_pool = once("rot_ready"), once("hid_by_pool")
        q_parts, k_parts, qk_out = once("q_parts"), once("k_parts"), once("qk_out")
        stacks = [once(f"stack{n}") for n in range(SETS)]
        nm_ready, m_in = once("nm_ready"), once("m_in")
        p_used = once("p_used")
        rd_ready, yn_ready = once("rd_ready"), once("yn_ready")
        base_ready, xhi_ready, xlo_ready = once("base_ready"), once("xhi_ready"), once("xlo_ready")
        lge_ready, rw_ready, rw_out = once("lge_ready"), once("rw_ready"), once("rw_out")
        segments = [[] for _ in range(NM)]
        for e in range(NE):
            at = e * HID
            while at < (e + 1) * HID:
                end = min((e + 1) * HID, (at // 128 + 1) * 128)
                segments[at // 128].append((at % 128, at % 128 + end - at, e))
                at = end
        wb_in = [once(f"wb_in{m}") for m in range(NM)]
        gate_ready, hid_ready, hid_used = once("gate_ready"), once("hid_ready"), once("hid_used")
        stored = once("stored")
        idle_made = once("idle_made")
        conv_in = [once(f"conv_in_{n}") for n in ("real", "imag")]
        phase_in, norm_in, lin_in, attn_in, moe_in = (
            once(n) for n in ("phase_in", "norm_in", "lin_in", "attn_in", "moe_in"))
        x_loaded = [[once(f"x_loaded{g}{a}") for a in range(2)] for g in range(PAIRS)]
        pool_made, dve_made, wb_made = once("pool_made"), once("dve_made"), once("wb_made")
        wsplit, sines, conv_w = once("wsplit"), once("sines"), once("conv_w")

        block = ctx.enter_context(nc.Block())

        norm_consts = [(center[:], cen), (average[:], avg)]
        lin_consts = [(lin_ws[:], lin_w), (lin_b[:], lin_bqk), (lin_vb[:], lin_bv), (q_decay[:], qdec),
                      (k_decay[:], kdec)]
        attn_consts = [(ln_ws[:], ln_w), (qkv_ws[:], qkv_w), (q_cos[:], qcos), (q_sin[:], qsin), (k_tab[:], ktab),
                       (ident[:], eye), (den_sel[:], dsel), (wo_ws[:], wo_w), (router_ws[:], router_w),
                       (rank_t[:], rank)]
        moe_consts = [(raw[0], w1T), (raw[1], w3T), (w2_ws[:].rearrange("p m c -> p (m c)"), w2T)]
        POOL_MADE, DVE_MADE = 21, 9

        def banks(step):
            return work[:, plan[step][0]:plan[step][0] + 1 + wide(step)]

        def wait_free(step):
            for before in plan[step][2]:
                wait_read(nc.tensor, before)

        def wait_full(eng, step):
            bank, use, _ = plan[step]
            eng.wait_ge(full[bank], use + 1)

        def wait_read(eng, step):
            bank, use, _ = plan[step]
            eng.wait_ge(free[bank], use + 1)

        def full_of(step):
            return full[plan[step][0]]

        def free_of(step):
            return free[plan[step][0]]

        def halves(tile):
            return tile[:, 0:T].rearrange("p (a t) -> p a t", a=2)

        def moe_index(g, c, m, b):
            return ((2 * g + c) * NM + m) * 2 + b

        MOE = [s for s in STEPS if s[0] == "moe"]

        def by_pool(n):
            return n % POOL_TAKES == POOL_TAKES - 1

        def wait_hidden(eng, n):
            if (n + 1) // POOL_TAKES:
                eng.wait_ge(hid_by_pool, (n + 1) // POOL_TAKES)
            eng.wait_ge(hid_ready, n + 1 - (n + 1) // POOL_TAKES)

        def load_x(eng, g, a):
            t0, t1 = ((0, HALF + TAPS), (HALF + TAPS, XW))[a]
            for r in range(2):
                eng.dma_start(x_in[g][64 * r:64 * r + 64, :, t0:t1],
                              xT[2 * g:2 * g + 2, :, r + t0:r + t1].rearrange("b c t -> c b t"))\
                   .then_inc(x_loaded[g][a], 16)

        def load_routes(sp, g, c, m):
            for r0, r1, e in segments[m]:
                sp.dma_start(wb[r0:r1, m, :, :],
                             w_scr[g, :, e, c * HALF:(c + 1) * HALF].unsqueeze(0).broadcast_to([r1 - r0, 2, HALF]))\
                  .then_inc(wb_in[m], 16)

        @block.sync
        def _(sp):
            sp.dma_start(phase[:], ph).then_inc(phase_in, 16)
            sp.dma_start(pt[4][:, 0:8 * C], wr).then_inc(conv_in[0], 16)
            sp.dma_start(pt[5][:, 0:8 * C], wi).then_inc(conv_in[1], 16)
            for g, a in ((0, 1), (1, 0), (1, 1)):
                load_x(sp, g, a)
            for tile, src in norm_consts:
                sp.dma_start(tile, src).then_inc(norm_in, 16)
            for tile, src in lin_consts:
                sp.dma_start(tile, src).then_inc(lin_in, 16)
            for tile, src in attn_consts:
                sp.dma_start(tile, src).then_inc(attn_in, 16)
            sp.wait_ge(pool_made, POOL_MADE)

            def load_stacks(bt):
                g, b, n = bt // 2, bt % 2, STACK[bt]
                for r in range(4):
                    rows = slice(16 * r, 16 * r + 16)
                    sp.dma_start(ks[n][rows].bitcast(f32), k_scr[g, r % 2, b].rearrange("h d t -> d h t"))\
                      .then_inc(stacks[n], 16)
                    sp.dma_start(qs[n][rows].bitcast(f32), q_scr[g, r // 2, b].rearrange("h d t -> d h t"))\
                      .then_inc(stacks[n], 16)
                sp.dma_start(qs[n][64:66].bitcast(f32), qs[n][66:68].bitcast(f32)).then_inc(stacks[n], 16)

            for step in STEPS:
                if step[0] == "v":
                    g = step[1]
                    for n in range(2):
                        sp.wait_ge(q_parts, 2 * g + n + 1)
                        sp.dma_start(q_scr[g, n].rearrange("b h d t -> (b h d) t"), parts[g][n][:].bitcast(f32))\
                          .then_inc(qk_out, 16)
                    for n in range(2):
                        sp.wait_ge(k_parts, 2 * g + n + 1)
                        sp.dma_start(k_scr[g, n].rearrange("b h d t -> (b h d) t"), kparts[n][:].bitcast(f32))\
                          .then_inc(qk_out, 16)
                    sp.wait_ge(qk_out, 64 * (g + 1))
                    for bt in ((0, 1) if g == 0 else (2,)):
                        load_stacks(bt)
                    if g:
                        for tile, src in moe_consts:
                            sp.dma_start(tile, src).then_inc(moe_in, 16)
                elif step[0] == "negmax":
                    bt = step[1]
                    wait_read(sp, step)
                    for hh in range(NH):
                        sp.dma_start(qs[STACK[bt]][64:66, hh, :].bitcast(f32), nrow[2 * hh:2 * hh + 2, 0:T])\
                          .then_inc(m_in, 16)
                elif step[0] == "y" and STACK[step[1]] in STACK[max(step[1] + 1, SETS):]:
                    wait_read(sp, ("score", step[1], NB - 1, NH - 1, 0))
                    load_stacks(STACK.index(STACK[step[1]], step[1] + 1))
                elif step[0] == "rwT":
                    g = step[1]
                    wait_read(sp, step)
                    sp.dma_start(w_scr[g].rearrange("b e t -> (b e) t"), r_wT[:, 0:T]).then_inc(rw_out, 16)
                    if g == 0:
                        sp.wait_ge(rw_out, 16)
                        for m in range(NM):
                            load_routes(sp, 0, 0, m)
                elif step[0] == "moe" and step[4] == 1:
                    g, c, m = step[1:4]
                    ahead = 2 * g + c + 1
                    if ahead < 2 * PAIRS:
                        if ahead == 2 and m == 0:
                            sp.wait_ge(rw_out, 32)
                        wait_hidden(sp, moe_index(g, c, m, 1))
                        load_routes(sp, ahead // 2, ahead % 2, m)
                elif step[0] == "outT":
                    g = step[1]
                    wait_read(sp, step)
                    for b in range(2):
                        o = o_t[g].rearrange("p i (b c) -> p i b c", b=2)
                        sp.dma_start(out[2 * g + b, 0:640, :].rearrange("(i q) c -> q i c", q=128), o[:, 0:5, b, :])\
                          .then_inc(stored, 16)
                        sp.dma_start(out[2 * g + b, 640:TV, :], o[0:TV - 640, 5, b, :]).then_inc(stored, 16)
            sp.wait_ge(stored, 64 * PAIRS)

        @block.gpsimd
        def _(pool):
            for tile in (eye_b, neg_qk):
                nc.gpsimd.memset(tile[:], 0.0).then_inc(pool_made, 1)
            for bt in range(B):
                nc.gpsimd.memset(v_aug[bt][:], 0.0).then_inc(pool_made, 1)
            for n in range(SETS):
                nc.gpsimd.memset(qs[n].bitcast(f32), 0.0).then_inc(pool_made, 1)
                nc.gpsimd.memset(ks[n].bitcast(f32), 0.0).then_inc(pool_made, 1)
            pool.wait_ge(pool_made, 12)
            nc.gpsimd.affine_select(out=eye_b[:], in_=eye_b[:], compare_op=ALU.not_equal, fill=1.0, base=0,
                                    pattern=[[-1, 128]], channel_multiplier=1).then_inc(pool_made, 1)
            nc.gpsimd.affine_select(out=neg_qk[:], in_=neg_qk[:], compare_op=ALU.is_ge, fill=NEG, base=0,
                                    pattern=[[-1, 128]], channel_multiplier=1).then_inc(pool_made, 1)
            for n in range(SETS):
                pool.wait_ge(pool_made, 14 + n)
                nc.gpsimd.memset(ks[n][64:66].bitcast(f32), 1.0).then_inc(pool_made, 1)
            pool.wait_ge(pool_made, 14 + SETS)
            for bt in range(B):
                nc.gpsimd.memset(v_aug[bt][:, :, :, HD:HD + 1], 1.0).then_inc(pool_made, 1)

            def causal(tile, j):
                part = tile[0:ROWS[j], 0:ROWS[j]]
                return nc.gpsimd.affine_select(out=part, in_=part, compare_op=ALU.is_ge, fill=0.0, base=0,
                                               pattern=[[1, ROWS[j]]], channel_multiplier=-1)

            for step in STEPS:
                if step[0] == "lin" and step[4] == 0:
                    _, g, j, b, k = step
                    wait_read(pool, step)
                    causal(p_lin[b], j).then_inc(pl_masked[b], 1)
                elif step[0] == "score" and step[4] == 0:
                    _, bt, j, hh, k = step
                    wait_read(pool, step)
                    causal(pt[((bt * NB + j) * NH + hh) % PT], j).then_inc(p_masked, 1)
                elif step == ("qperm", 1):
                    wait_read(pool, ("q", 1))
                    wait_read(pool, step)
                    nc.gpsimd.tensor_tensor(rot[1], tmp1[1], tmp2[1], ALU.add).then_inc(rot_ready, 1)
                    pool.wait_ge(rot_ready, 1)
                    nc.gpsimd.tensor_copy(parts[1][0][:], rot[1]).then_inc(q_parts, 1)
                    pool.wait_ge(q_parts, 3)
                    nc.gpsimd.tensor_tensor(parts[1][1][:], rot[1], parts[1][0][:].bitcast(f32), ALU.subtract)\
                        .then_inc(q_parts, 1)
                elif step == ("k", 1):
                    wait_read(pool, step)
                    nc.gpsimd.tensor_tensor(krot[1], kza[1][0:64], kzb[1][0:64], ALU.add).then_inc(rot_ready, 1)
                    pool.wait_ge(rot_ready, 2)
                    pool.wait_ge(qk_out, 64)
                    nc.gpsimd.tensor_copy(kparts[0][:], krot[1]).then_inc(k_parts, 1)
                    pool.wait_ge(k_parts, 3)
                    nc.gpsimd.tensor_tensor(kparts[1][:], krot[1], kparts[0][:].bitcast(f32), ALU.subtract)\
                        .then_inc(k_parts, 1)
                elif step[0] == "split":
                    low, n, at = step[1] // (2 * CUTS), step[1] // CUTS % 2, step[1] % CUTS * MP // CUTS
                    src, hi, lo = (tile[:, at:at + MP // CUTS] for tile in (raw[n], w_hi[n], w_lo[n]))
                    if step[1] == 0:
                        pool.wait_ge(moe_in, 16 * len(moe_consts))
                        wait_read(pool, ("score", STACK.index(SETS - 1), NB - 1, NH - 1, 0))
                    if low:
                        pool.wait_ge(wsplit, step[1] - 2 * CUTS + 1)
                        nc.gpsimd.tensor_tensor(lo, src, hi.bitcast(f32), ALU.subtract).then_inc(wsplit, 1)
                    else:
                        nc.gpsimd.tensor_copy(hi, src).then_inc(wsplit, 1)
                elif step[0] == "moe" and by_pool(moe_index(*step[1:])):
                    _, g, c, m, b = step
                    n = moe_index(g, c, m, b)
                    wait_read(pool, step)
                    pool.wait_ge(wb_in[m], (2 * g + c + 1) * 16 * len(segments[m]))
                    nc.gpsimd.tensor_tensor(hid[n % len(hid)], hid[n % len(hid)], wb[:, m, b, :], ALU.mult)\
                        .then_inc(hid_by_pool, 1)
                elif step[0] == "ms2":
                    g = step[1]
                    for b in range(2):
                        wait_read(pool, ("wo", 2 * g + b))
                    nc.gpsimd.tensor_tensor(h2[g], h2[g], x2[g], ALU.add).then_inc(base_ready, 1)

        @block.scalar
        def _(act):
            load_x(act, 0, 0)
            nc.scalar.preload_act_table_set("silu_and_others")
            act.wait_ge(trig_step, TRIG_STEPS)
            nc.scalar.activation(trig[:], trig[:], ACT.Sin).then_inc(sines, 1)
            nc.scalar.preload_act_table_set("natural_log_exp_and_others")
            act.wait_ge(dve_made, DVE_MADE)

            def square(src, dst, kind):
                nc.scalar.activation(dst[:, 0:T], src[:, 0:T], ACT.Square).then_inc(squared[kind], 1)

            def inverse_root(step, dst, which):
                wait_full(act, step)
                nc.scalar.activation(halves(dst), banks(step)[:, :, 0:HALF], ACT.Ln,
                                     bias=eps[:, which:which + 1]).then_inc(free_of(step), 1)
                wait_read(act, step)
                nc.scalar.activation(dst[:, 0:T], dst[:, 0:T], ACT.Exp, scale=-0.5).then_inc(rooted[step[0]], 1)

            silu_loaded = False
            for step in STEPS:
                kind = step[0]
                if silu_loaded and kind in ("den", "ms2", "router"):
                    nc.scalar.preload_act_table_set("natural_log_exp_and_others")
                    silu_loaded = False
                if kind == "conv":
                    wait_full(act, step)
                    _, g, a = step
                    nc.scalar.activation(halves(h[g])[:, a], banks(step)[:, 0, 0:HALF], ACT.Copy)\
                      .then_inc(free_of(step), 1)
                elif kind in ("cen1", "cen2"):
                    g = step[1]
                    wait_full(act, step)
                    nc.scalar.activation(halves(sq[g]), banks(step)[:, :, 0:HALF], ACT.Square)\
                      .then_inc(squared["var" + kind[-1]], 1)
                    nc.scalar.activation(halves(cent[g]), banks(step)[:, :, 0:HALF], ACT.Copy)\
                      .then_inc(free_of(step), 1)
                elif kind in ("var1", "var2"):
                    inverse_root(step, rs[step[1]], 0)
                elif kind == "ms1":
                    g = step[1]
                    act.wait_ge(normed["var2"], g + 1)
                    square(x2[g], sq[g], kind)
                    inverse_root(step, rs[g], 1)
                elif kind == "lin":
                    _, g, j, b, k = step
                    wait_full(act, step)
                    if k == 0 and g * NB + j:
                        act.wait_ge(pl_used[b], g * NB + j)
                    o, w = pieces(WIDTH[j])[k]
                    nc.scalar.activation(p_lin[b][0:ROWS[j], o:o + w], banks(step)[0:ROWS[j], 0, 0:w], ACT.Copy)\
                      .then_inc(free_of(step), 1)
                elif kind == "v":
                    g = step[1]
                    if g == 0:
                        act.wait_ge(pool_made, POOL_MADE)
                    wait_full(act, step)
                    vals = banks(step)[:, 0, 0:NB * 64].rearrange("p (i b h d) -> p i b h d", i=NB, b=2, h=NKV)
                    for b in range(2):
                        for i0, i1, m in ((0, NB - 1, 128), (NB - 1, NB, ROWS[-1])):
                            last = nc.scalar.activation(v_aug[2 * g + b][0:m, i0:i1, :, 0:HD], vals[0:m, i0:i1, b],
                                                        ACT.Copy)
                            last.then_inc(free_of(step) if (b, i0) == (1, NB - 1) else va_first, 1)
                elif kind == "negmax":
                    wait_full(act, step)
                    if step[1]:
                        act.wait_ge(m_in, 64 * step[1])
                    nc.scalar.activation(nrow.rearrange("p (a t) -> p a t", a=2), banks(step)[0:2 * NH, :, 0:384],
                                         ACT.Copy).then_inc(free_of(step), 1)
                elif kind == "score":
                    _, bt, j, hh, k = step
                    n = (bt * NB + j) * NH + hh
                    wait_full(act, step)
                    if k == 0 and n >= PT:
                        act.wait_ge(p_used, (n - PT) // NH + 1)
                    o, w = pieces(WIDTH[j])[k]
                    nc.scalar.activation(pt[n % PT][0:ROWS[j], o:o + w], banks(step)[0:ROWS[j], 0, 0:w], ACT.Exp)\
                      .then_inc(free_of(step), 1)
                elif kind == "y":
                    bt = step[1]
                    act.wait_ge(p_used, NB * (bt + 1))
                    if bt:
                        act.wait_ge(yn_ready, bt)
                    nc.scalar.activation(halves(ysb), acc[:, :, 0:HALF], ACT.Copy).then_inc(acc_out, 1)
                elif kind == "den":
                    wait_full(act, step)
                    nc.scalar.activation(halves(rden), banks(step)[:, :, 0:HALF], ACT.Ln).then_inc(free_of(step), 1)
                    wait_read(act, step)
                    nc.scalar.activation(rden, rden, ACT.Exp, scale=-1.0).then_inc(rd_ready, 1)
                elif kind == "ms2":
                    g = step[1]
                    for b in range(2):
                        wait_read(act, ("wo", 2 * g + b))
                    if g:
                        act.wait_ge(flat_ready, g)
                    square(x2[g], rs2, kind)
                    inverse_root(step, rs2, 1)
                elif kind == "router":
                    g = step[1]
                    act.wait_ge(flat_ready, g + 1)
                    for b in range(2):
                        rows = slice(64 * b, 64 * b + 64)
                        nc.scalar.activation(xs[g][b][rows], flat[rows, 0:T], ACT.Copy).then_inc(xhi_ready, 1)
                    wait_read(act, step)
                    nc.scalar.activation(ta[:], lg[:], ACT.Exp).then_inc(lge_ready, 1)
                elif kind == "rwT":
                    wait_full(act, step)
                    if step[1]:
                        act.wait_ge(rw_out, 16 * step[1])
                    nc.scalar.activation(r_wT.rearrange("p (a t) -> p a t", a=2), banks(step)[0:2 * NE, :, 0:384],
                                         ACT.Copy).then_inc(free_of(step), 1)
                elif kind == "moe":
                    n = moe_index(*step[1:])
                    silu_loaded = True
                    wait_full(act, step)
                    if n >= 4:
                        wait_read(act, MOE[n - 4])
                    nc.scalar.activation(gate[n % 4], banks(step)[:, 0, 0:HALF], ACT.Silu).then_inc(gate_ready, 1)
                elif kind == "outT":
                    g = step[1]
                    wait_full(act, step)
                    nc.scalar.activation(o_t[g].rearrange("p (a i) c -> p a (i c)", a=2),
                                         banks(step)[:, :, 0:384], ACT.Copy).then_inc(free_of(step), 1)

        @block.vector
        def _(v):
            nc.vector.memset(idle, 0.0).then_inc(idle_made, 1)
            v.wait_ge(phase_in, 16)
            steps = [0]

            def trig_link(ins):
                steps[0] += 1
                ins.then_inc(trig_step, 1)
                v.wait_ge(trig_step, steps[0])

            trig_link(nc.vector.tensor_scalar(trig[:, 0, :], phase[:], float(np.pi / 2), None, ALU.add))
            trig_link(nc.vector.tensor_copy(trig[:, 1, :], phase[:]))
            trig_link(nc.vector.tensor_scalar(turns[:], trig[:], float(1 / (2 * np.pi)), ROUND, ALU.mult, ALU.add))
            trig_link(nc.vector.tensor_scalar(turns[:], turns[:], ROUND, None, ALU.subtract))
            trig_link(nc.vector.scalar_tensor_tensor(out=trig[:], in0=turns[:], scalar=-6.28125, in1=trig[:],
                                                     op0=ALU.mult, op1=ALU.add))
            trig_link(nc.vector.scalar_tensor_tensor(out=trig[:], in0=turns[:], scalar=-(2 * np.pi - 6.28125),
                                                     in1=trig[:], op0=ALU.mult, op1=ALU.add))
            trig_link(nc.vector.tensor_scalar(trig[:], trig[:], 3.1415925, -3.1415925, ALU.min, ALU.max))
            assert steps[0] == TRIG_STEPS
            v.wait_ge(sines, 1)
            for tile, n in ((w_real, 0), (w_imag, 1)):
                v.wait_ge(conv_in[n], 16)
                nc.vector.tensor_tensor(tile, tile, trig[:, n, :].unsqueeze(2).broadcast_to([128, 8, C]),
                                        ALU.mult).then_inc(conv_w, 1)
            v.wait_ge(conv_w, 2)
            for n in range(2):
                taps = slice(4 * n, 4 * n + 4)
                nc.vector.tensor_tensor(w_conv[:, taps], w_real[:, taps], w_imag[:, taps], ALU.subtract)\
                  .then_inc(conv_w, 1)
            nc.vector.memset(kz[0][0], 0.0).then_inc(dve_made, 1)
            nc.vector.memset(kz[0][1], 0.0).then_inc(dve_made, 1)
            nc.vector.memset(kz[1][0], 0.0).then_inc(dve_made, 1)
            nc.vector.memset(kz[1][1], 0.0).then_inc(dve_made, 1)
            for tile in h:
                nc.vector.memset(tile[:, T:TP], 0.0).then_inc(dve_made, 1)
            nc.vector.memset(smax[:], 0.0).then_inc(dve_made, 1)
            nc.vector.memset(eps[:, 0:1], 1e-5).then_inc(dve_made, 1)
            nc.vector.memset(eps[:, 1:2], 1e-6).then_inc(dve_made, 1)
            chain = [0]

            def link(ins):
                chain[0] += 1
                ins.then_inc(dve_step, 1)
                v.wait_ge(dve_step, chain[0])

            def add(ins):
                chain[0] += 1
                ins.then_inc(dve_step, 1)

            def over_experts(stat):
                return stat[:].unsqueeze(2).broadcast_to([128, 2 * NB, NE])

            def weigh(n):
                _, g, c, m, b = MOE[n]
                if by_pool(n):
                    return
                wait_read(v, MOE[n])
                if not b:
                    v.wait_ge(wb_in[m], (2 * g + c + 1) * 16 * len(segments[m]))
                nc.vector.tensor_tensor(hid[n % len(hid)], hid[n % len(hid)], wb[:, m, b, :], ALU.mult).then_inc(hid_ready, 1)

            for step in STEPS:
                kind, g = step[0], step[1] if len(step) > 1 else None
                if kind in ("var1", "var2"):
                    wait_read(v, ("cen" + kind[-1], g))
                    v.wait_ge(rooted[kind], g + 1)
                    nc.vector.tensor_tensor((xn if kind == "var1" else x2)[g], cent[g], rs[g], ALU.mult)\
                      .then_inc(normed[kind], 1)
                    if kind == "var2" and g == 0:
                        v.wait_ge(attn_in, 16 * len(attn_consts))
                    if kind == "var1" and g == 0:
                        v.wait_ge(lin_in, 16 * len(lin_consts))
                elif kind == "linq":
                    wait_full(v, step)
                    nc.vector.scalar_tensor_tensor(
                        out=halves(tmp1[g]), in0=banks(step)[:, :, 0:HALF], scalar=lin_b[:, 0:1],
                        in1=halves(q_decay), op0=ALU.add, op1=ALU.mult).then_inc(free_of(step), 1)
                elif kind == "link":
                    wait_full(v, step)
                    for b in range(2):
                        rows = slice(64 * b, 64 * b + 64)
                        nc.vector.scalar_tensor_tensor(
                            out=halves(kz[g][b])[rows], in0=banks(step)[rows, :, 0:HALF], scalar=lin_b[rows, 1:2],
                            in1=halves(k_decay)[rows], op0=ALU.add, op1=ALU.mult)\
                          .then_inc(free_of(step) if b else kz_first, 1)
                elif kind == "linv":
                    wait_full(v, step)
                    for i0, i1, m in ((0, 3, 128), (3, 5, 128), (5, 6, ROWS[-1])):
                        a = i0 // 3
                        nc.vector.tensor_tensor(
                            v_lin[g][0:m, i0:i1, :],
                            banks(step)[0:m, a, 128 * (i0 - 3 * a):128 * (i1 - 3 * a)].rearrange(
                                "p (i c) -> p i c", i=i1 - i0),
                            lin_vb[0:m].unsqueeze(1).broadcast_to([m, i1 - i0, 128]), ALU.add)\
                          .then_inc(free_of(step) if i0 == 5 else vl_first, 1)
                elif kind == "h2":
                    for b in range(2):
                        v.wait_ge(pl_used[b], NB * (g + 1))
                    nc.vector.tensor_tensor(halves(h2[g]), acc[:, :, 0:HALF], halves(h[g]), ALU.add).then_inc(acc_out, 1)
                elif kind == "ms1":
                    v.wait_ge(rooted[kind], g + 1)
                    nc.vector.scalar_tensor_tensor(out=xn[g], in0=x2[g], scalar=ln_ws[:, 0:1], in1=rs[g],
                                                   op0=ALU.mult, op1=ALU.mult).then_inc(xn2_ready, 1)
                elif kind == "q":
                    wait_full(v, step)
                    nc.vector.tensor_tensor(halves(tmp1[g]), banks(step)[:, :, 0:HALF], halves(q_cos), ALU.mult)\
                      .then_inc(free_of(step), 1)
                elif kind == "qperm":
                    wait_full(v, step)
                    nc.vector.tensor_tensor(halves(tmp2[g]), banks(step)[:, :, 0:HALF], halves(q_sin), ALU.mult)\
                      .then_inc(free_of(step), 1)
                    if g == 0:
                        wait_read(v, step)
                        link(nc.vector.tensor_tensor(rot[g], tmp1[g], tmp2[g], ALU.add))
                        nc.vector.tensor_copy(parts[g][0][:], rot[g]).then_inc(q_parts, 1)
                        v.wait_ge(q_parts, 1)
                        nc.vector.tensor_tensor(parts[g][1][:], rot[g], parts[g][0][:].bitcast(f32), ALU.subtract)\
                          .then_inc(q_parts, 1)
                elif kind == "k":
                    wait_full(v, step)
                    link(nc.vector.tensor_tensor(halves(kza[g])[0:64], banks(step)[0:64, :, 0:HALF],
                                                 halves(k_tab)[0:64], ALU.mult))
                    nc.vector.tensor_tensor(halves(kzb[g])[0:64], banks(step)[64:128, :, 0:HALF],
                                            halves(k_tab)[64:128], ALU.mult).then_inc(free_of(step), 1)
                    if g == 0:
                        wait_read(v, step)
                        link(nc.vector.tensor_tensor(krot[g], kza[g][0:64], kzb[g][0:64], ALU.add))
                        nc.vector.tensor_copy(kparts[0][:], krot[g]).then_inc(k_parts, 1)
                        v.wait_ge(k_parts, 1)
                        nc.vector.tensor_tensor(kparts[1][:], krot[g], kparts[0][:].bitcast(f32), ALU.subtract)\
                          .then_inc(k_parts, 1)
                elif kind == "v" and g == 1:
                    wait_full(v, step)
                    nc.vector.memset(wb_space[:, NM - 1, :], 0.0).then_inc(wb_made, 1)
                elif kind == "max":
                    i, w, heads = ROUNDS[step[2]]
                    m = ROWS[i]
                    wait_full(v, step)
                    to = smax[0:m, i, heads[0]:heads[-1] + 1]
                    if w > 512:
                        src, axis = banks(step)[0:m, 0:2, 0:w // 2], AX.XY
                    else:
                        src, axis = banks(step)[0:m, 0, 0:len(heads) * w].rearrange("p (g s) -> p g s", s=w), AX.X
                    nc.vector.tensor_reduce(to, src, axis, ALU.max).then_inc(free_of(step), 1)
                elif kind == "negmax":
                    bt = step[1]
                    wait_read(v, ("max", bt, len(ROUNDS) - 1))
                    if bt:
                        wait_full(v, ("negmax", bt - 1))
                    link(nc.vector.tensor_scalar(nmh[:], smax[:], -1.0, None, ALU.mult))
                    nc.vector.tensor_copy(nmx[:, :, :, 0], nmh[:].bitcast(f32)).then_inc(nm_ready, 1)
                    nc.vector.scalar_tensor_tensor(out=nmx[:, :, :, 1], in0=smax[:], scalar=-1.0,
                                                   in1=nmh[:].bitcast(f32), op0=ALU.mult, op1=ALU.subtract)\
                      .then_inc(nm_ready, 1)
                elif kind == "wo":
                    bt = step[1]
                    rows, res = slice(64 * (bt % 2), 64 * (bt % 2) + 64), halves(x2[bt // 2])
                    v.wait_ge(rd_ready, bt + 1)
                    nc.vector.tensor_tensor(yn, ysb, rden, ALU.mult).then_inc(yn_ready, 1)
                    wait_full(v, step)
                    nc.vector.tensor_tensor(res[rows], banks(step)[rows, :, 0:HALF], res[rows], ALU.add)\
                      .then_inc(free_of(step), 1)
                elif kind == "ms2":
                    if g:
                        v.wait_ge(xhi_ready, 2 * g)
                    v.wait_ge(rooted[kind], g + 1)
                    nc.vector.scalar_tensor_tensor(out=flat[:, 0:T], in0=x2[g], scalar=ln_ws[:, 1:2], in1=rs2,
                                                   op0=ALU.mult, op1=ALU.mult).then_inc(flat_ready, 1)
                elif kind == "router":
                    logits = banks(step)[:, 0, 0:2 * NB * NE].rearrange("p (g e) -> p g e", e=NE)
                    wait_full(v, step)
                    link(nc.vector.tensor_reduce(s1[:], logits, AX.X, ALU.max))
                    nc.vector.tensor_tensor(lg[:], logits, over_experts(s1), ALU.subtract).then_inc(free_of(step), 1)
                elif kind == "xlo":
                    b = step[2]
                    rows, other = slice(64 * b, 64 * b + 64), slice(64 - 64 * b, 128 - 64 * b)
                    v.wait_ge(xhi_ready, 2 * g + b + 1)
                    nc.vector.tensor_tensor(xs[g][b][other], flat[rows, 0:T], xs[g][b][rows].bitcast(f32),
                                            ALU.subtract).then_inc(xlo_ready, 1)
                elif kind == "top":
                    v.wait_ge(dve_step, chain[0])
                    k = step[2]
                    ranks = rank_t[:].unsqueeze(1).broadcast_to([128, 2 * NB, NE])
                    if k == 0:
                        v.wait_ge(lge_ready, g + 1)
                        link(nc.vector.tensor_reduce(s1[:], ta[:], AX.X, ALU.add))
                        add(nc.vector.reciprocal(s2[:], s1[:]))
                    elif k == 1:
                        link(nc.vector.tensor_tensor(lg[:], ta[:], over_experts(s2), ALU.mult))
                        add(nc.vector.tensor_reduce(s1[:], lg[:], AX.X, ALU.max))
                    elif k in (2, 6):
                        src, top = (lg, s1) if k == 2 else (ta, s2)
                        link(nc.vector.tensor_tensor(tb[:], src[:], over_experts(top), ALU.is_equal))
                        add(nc.vector.tensor_tensor(tb[:], tb[:], ranks, ALU.mult))
                    elif k in (3, 7):
                        link(nc.vector.tensor_reduce(s3[:], tb[:], AX.X, ALU.max))
                        add(nc.vector.tensor_tensor((oh if k == 3 else tb)[:], tb[:], over_experts(s3), ALU.is_equal))
                    elif k == 4:
                        add(nc.vector.scalar_tensor_tensor(out=ta[:], in0=oh[:], scalar=-2.0, in1=lg[:],
                                                           op0=ALU.mult, op1=ALU.add))
                    elif k == 5:
                        add(nc.vector.tensor_reduce(s2[:], ta[:], AX.X, ALU.max))
                    elif k == 8:
                        link(nc.vector.tensor_tensor(oh[:], oh[:], tb[:], ALU.add))
                        add(nc.vector.tensor_tensor(oh[:], oh[:], lg[:], ALU.mult))
                    elif k == 9:
                        link(nc.vector.scalar_tensor_tensor(out=s1[:], in0=s1[:], scalar=1e-9, in1=s2[:],
                                                            op0=ALU.add, op1=ALU.add))
                        add(nc.vector.reciprocal(s3[:], s1[:]))
                    elif k == 10:
                        nc.vector.tensor_tensor(ta[:], oh[:], over_experts(s3), ALU.mult).then_inc(rw_ready, 1)
                elif kind == "moe":
                    n = moe_index(*step[1:])
                    v.wait_ge(gate_ready, n + 1)
                    if n >= len(hid):
                        v.wait_ge(hid_used, (n - len(hid)) // 2 + 1)
                    nc.vector.tensor_tensor(hid[n % len(hid)], banks(step)[:, 1, 0:HALF], gate[n % 4], ALU.mult)\
                      .then_inc(free_of(step), 1)
                    if n:
                        weigh(n - 1)
                elif kind == "last":
                    weigh(len(MOE) - 1)
                elif kind == "fin":
                    _, g, c = step
                    v.wait_ge(base_ready, g + 1)
                    v.wait_ge(hid_used, (2 * g + c + 1) * NM)
                    nc.vector.tensor_tensor(halves(fin[g])[:, c], acc[:, c, 0:HALF], halves(h2[g])[:, c], ALU.add)\
                      .then_inc(acc_out, 1)

        @block.tensor
        def _(pe):
            pe.wait_ge(idle_made, 1)
            for _ in range(IDLE_PRODUCTS):
                nc.tensor.matmul(acc[:, 0, :], idle[:, 0:128], idle, start=True, stop=True)
            pe.wait_ge(conv_w, 3)

            def mix(step, weights, src):
                wait_free(step)
                for a in range(2):
                    last = nc.tensor.matmul(banks(step)[:, a, 0:HALF], weights, halves(src)[:, a],
                                            start=True, stop=True)
                last.then_inc(full_of(step), 1)

            def down(n):
                g, c, m = MOE[2 * n][1:4]
                wait_hidden(pe, 2 * n + 1)
                for b in range(2):
                    last = nc.tensor.matmul(acc[64 * b:64 * b + 64, c, 0:HALF], w2_ws[:, m, :],
                                            hid[(2 * n + b) % len(hid)], start=(m == 0), stop=(m == NM - 1))
                last.then_inc(hid_used, 1)

            for step in STEPS:
                kind, g = step[0], step[1] if len(step) > 1 else None
                if kind == "conv":
                    wait_free(step)
                    pe.wait_ge(x_loaded[g][step[2]], 32)
                    a = step[2]
                    for j in range(TAPS // 2):
                        if (g, a, j) == (0, 0, 4):
                            pe.wait_ge(conv_w, 4)
                        for b in range(2):
                            last = nc.tensor.matmul(banks(step)[64 * b:64 * b + 64, 0, 0:HALF], w_conv[:, j, :],
                                                    x_in[g][:, b, 2 * j + HALF * a:2 * j + HALF * (a + 1)],
                                                    start=(j == 0), stop=(j == TAPS // 2 - 1))
                    last.then_inc(full_of(step), 1)
                elif kind == "cen1":
                    if g == 0:
                        pe.wait_ge(norm_in, 32)
                    wait_read(pe, ("conv", g, 0))
                    wait_read(pe, ("conv", g, 1))
                    mix(step, center[:], h[g])
                elif kind == "cen2":
                    pe.wait_ge(acc_out, ACC_OUT["h2", g])
                    mix(step, center[:], h2[g])
                elif kind in ("var1", "var2", "ms1", "ms2"):
                    pe.wait_ge(squared[kind], g + 1)
                    mix(step, average[:], rs2 if kind == "ms2" else sq[g])
                elif kind in ("linq", "link"):
                    if kind == "linq":
                        if g == 0:
                            pe.wait_ge(lin_in, 16 * len(lin_consts))
                        pe.wait_ge(normed["var1"], g + 1)
                    mix(step, lin_ws[:, 0 if kind == "linq" else 1, :], xn[g])
                elif kind == "linv":
                    wait_free(step)
                    for i in range(NB):
                        last = nc.tensor.matmul(banks(step)[0:ROWS[i], i // 3, 128 * (i % 3):128 * (i % 3) + 128],
                                                xn[g][:, 128 * i:128 * i + ROWS[i]], lin_ws[:, 2, :],
                                                start=True, stop=True)
                    last.then_inc(full_of(step), 1)
                elif kind == "lin":
                    _, g, j, b, k = step
                    if (j, b, k) == (0, 0, 0):
                        wait_read(pe, ("linq", g))
                        pe.wait_ge(kz_first, g + 1)
                        wait_read(pe, ("link", g))
                    wait_free(step)
                    o, w = pieces(WIDTH[j])[k]
                    nc.tensor.matmul(banks(step)[0:ROWS[j], 0, 0:w], kz[g][b][:, 128 * j:128 * j + ROWS[j]],
                                     tmp1[g][:, 128 * j + o:128 * j + o + w], start=True, stop=True)\
                      .then_inc(full_of(step), 1)
                elif kind == "lv":
                    j = step[2]
                    if j == 0:
                        pe.wait_ge(vl_first, 2 * g + 2)
                        wait_read(pe, ("linv", g))
                        if g:
                            pe.wait_ge(acc_out, ACC_OUT["h2", g - 1])
                    for b in range(2):
                        pe.wait_ge(pl_masked[b], g * NB + j + 1)
                        wait_read(pe, ("lin", g, j, b, len(pieces(WIDTH[j])) - 1))
                        for a, t0, t1 in spans(j):
                            last = nc.tensor.matmul(acc[64 * b:64 * b + 64, a, t0 - a * HALF:t1 - a * HALF],
                                                    v_lin[g][0:ROWS[j], j, 64 * b:64 * b + 64],
                                                    p_lin[b][0:ROWS[j], t0 - 128 * j:t1 - 128 * j],
                                                    start=(j == 0), stop=(j == NB - 1 or (a == 0 and j == 2)))
                        last.then_inc(pl_used[b], 1)
                elif kind in ("q", "qperm", "k"):
                    if kind == "q":
                        if g == 0:
                            pe.wait_ge(attn_in, 16 * len(attn_consts))
                        pe.wait_ge(xn2_ready, g + 1)
                    n = ("q", "qperm", "k").index(kind)
                    mix(step, qkv_ws[:, 128 * n:128 * n + 128], xn[g])
                elif kind == "v":
                    wait_free(step)
                    for i in range(NB):
                        last = nc.tensor.matmul(banks(step)[0:ROWS[i], 0, 64 * i:64 * i + 64],
                                                xn[g][:, 128 * i:128 * i + ROWS[i]], qkv_ws[:, 384:448],
                                                start=True, stop=True)
                    last.then_inc(full_of(step), 1)
                elif kind == "max":
                    bt = step[1]
                    i, w, heads = ROUNDS[step[2]]
                    b, m, cut = STACK[bt], ROWS[i], pieces(w)
                    if step[2] == 0:
                        pe.wait_ge(stacks[b], 144 * (1 + (b in STACK[:bt])))
                        if bt == 0:
                            pe.wait_ge(pool_made, POOL_MADE)
                    wait_free(step)
                    for n, hh in enumerate(heads):
                        for k, (o, cw) in enumerate(cut):
                            bank, col = k, n * w
                            diag = k == len(cut) - 1
                            nc.tensor.matmul(banks(step)[0:m, bank, col:col + cw],
                                             qs[b][:, hh, 128 * i:128 * i + m], ks[b][:, hh // 2, o:o + cw],
                                             start=True, stop=not diag)
                            if diag:
                                last = nc.tensor.matmul(banks(step)[0:m, bank, col + cw - m:col + cw],
                                                        eye_b[:, 0:m], neg_qk[:, 0:m], start=False, stop=True)
                    last.then_inc(full_of(step), 1)
                elif kind == "negmax":
                    pe.wait_ge(nm_ready, 2 * step[1] + 2)
                    wait_free(step)
                    for i in range(NB):
                        last = nc.tensor.matmul(banks(step)[0:2 * NH, i // 3, 128 * (i % 3):128 * (i % 3) + 128],
                                                nmx[0:ROWS[i], i].rearrange("p h n -> p (h n)"),
                                                ident[0:ROWS[i], :], start=True, stop=True)
                    last.then_inc(full_of(step), 1)
                elif kind == "score":
                    _, bt, j, hh, k = step
                    b = STACK[bt]
                    if (j, hh, k) == (0, 0, 0):
                        pe.wait_ge(m_in, 64 * (bt + 1))
                    wait_free(step)
                    o, w = pieces(WIDTH[j])[k]
                    nc.tensor.matmul(banks(step)[0:ROWS[j], 0, 0:w], ks[b][:, hh // 2, 128 * j:128 * j + ROWS[j]],
                                     qs[b][:, hh, 128 * j + o:128 * j + o + w], start=True, stop=True)\
                      .then_inc(full_of(step), 1)
                elif kind == "pv":
                    _, bt, j = step
                    if j == 0:
                        if bt % 2 == 0:
                            pe.wait_ge(va_first, 3 * (bt // 2 + 1))
                            wait_read(pe, ("v", bt // 2))
                        pe.wait_ge(acc_out, ACC_OUT["y", bt] - 1)
                    for hh in range(NH):
                        n = (bt * NB + j) * NH + hh
                        pe.wait_ge(p_masked, n + 1)
                        wait_read(pe, ("score", bt, j, hh, len(pieces(WIDTH[j])) - 1))
                        for a, t0, t1 in spans(j):
                            last = nc.tensor.matmul(
                                acc[32 * hh:32 * hh + 32, a, t0 - a * HALF:t1 - a * HALF],
                                v_aug[bt][0:ROWS[j], j, hh // 2, :],
                                pt[n % PT][0:ROWS[j], t0 - 128 * j:t1 - 128 * j],
                                start=(j == 0), stop=(j == NB - 1 or (a == 0 and j == 2)))
                    last.then_inc(p_used, 1)
                elif kind == "den":
                    pe.wait_ge(acc_out, ACC_OUT["y", step[1]])
                    mix(step, den_sel[:], ysb)
                elif kind == "wo":
                    b = step[1] % 2
                    wait_free(step)
                    pe.wait_ge(yn_ready, step[1] + 1)
                    for a in range(2):
                        last = nc.tensor.matmul(banks(step)[64 * b:64 * b + 64, a, 0:HALF], wo_ws[:], halves(yn)[:, a],
                                                start=True, stop=True)
                    last.then_inc(full_of(step), 1)
                elif kind == "router":
                    pe.wait_ge(flat_ready, g + 1)
                    wait_free(step)
                    for i in range(NB):
                        last = nc.tensor.matmul(banks(step)[:, 0, 2 * NE * i:2 * NE * (i + 1)],
                                                flat[:, 128 * i:128 * i + 128], router_ws[:], start=True, stop=True)
                    last.then_inc(full_of(step), 1)
                elif kind == "rwT":
                    pe.wait_ge(rw_ready, g + 1)
                    wait_free(step)
                    for i in range(NB):
                        last = nc.tensor.matmul(banks(step)[0:2 * NE, i // 3, 128 * (i % 3):128 * (i % 3) + 128],
                                                ta[:, 2 * i:2 * i + 2, :].rearrange("p b e -> p (b e)"), ident[:],
                                                start=True, stop=True)
                    last.then_inc(full_of(step), 1)
                elif kind == "moe":
                    _, g, c, m, b = step
                    n = moe_index(g, c, m, b)
                    if (c, m, b) == (0, 0, 0):
                        pe.wait_ge(xhi_ready, 2 * g + 2)
                        pe.wait_ge(xlo_ready, 2 * g + 2)
                        if g == 0:
                            pe.wait_ge(wsplit, 4 * CUTS)
                    wait_free(step)
                    for k in range(2):
                        for part in (w_hi, w_lo):
                            last = nc.tensor.matmul(banks(step)[:, k, 0:HALF], part[k][:, 128 * m:128 * m + 128],
                                                    halves(xs[g][b])[:, c], start=(part is w_hi), stop=(part is w_lo))
                    last.then_inc(full_of(step), 1)
                    if b and n // 2 >= LAG:
                        lagged = n // 2 - LAG
                        if lagged % NM == 0:
                            before = ACC_OUT["y", B - 1] if lagged < 2 * NM else ACC_OUT["fin", 0, lagged // NM - 2]
                            pe.wait_ge(acc_out, before)
                        down(lagged)
                elif kind == "last":
                    for n in range(len(MOE) // 2 - LAG, len(MOE) // 2):
                        down(n)
                elif kind == "outT":
                    pe.wait_ge(acc_out, ACC_OUT["fin", g, 1])
                    wait_free(step)
                    for i in range(NB):
                        last = nc.tensor.transpose(banks(step)[:, i // 3, 128 * (i % 3):128 * (i % 3) + 128],
                                                   fin[g][:, 128 * i:128 * i + 128], ident[:])
                    last.then_inc(full_of(step), 1)


_OUT = (B, TV, C)


def _layouts(inputs):
    f = np.float32
    a = {k: np.asarray(v) for k, v in inputs.items()}

    def twice(w):
        z = np.zeros((2 * w.shape[0], 2 * w.shape[1]), f)
        z[:w.shape[0], :w.shape[1]] = w
        z[w.shape[0]:, w.shape[1]:] = w
        return z

    got = {}
    x = np.zeros((B, C, XW + 1), f)
    x[..., :S_IN] = a["x"].transpose(0, 2, 1)
    got["xT"] = x
    for name, key in (("wr", "L0_tok_w_real"), ("wi", "L0_tok_w_imag")):
        w = a[key].transpose(2, 1, 0).reshape(TAPS // 2, 2, C, C)
        got[name] = w.transpose(1, 2, 0, 3).reshape(128, -1)
    got["ph"] = np.repeat(a["L0_tok_phases"].reshape(TAPS // 2, 2).T, 64, axis=0)
    w, bias = a["L0_attn_Wqkv"], a["L0_attn_bqkv"]
    got["lin_w"] = np.stack([twice(w[:, 64 * n:64 * n + 64]) for n in range(3)], axis=1)
    got["lin_bqk"] = np.stack([np.tile(bias[64 * n:64 * n + 64], 2) for n in range(2)], axis=1)
    got["lin_bv"] = np.broadcast_to(np.tile(bias[128:192], 2), (128, 128))
    got["ln_w"] = np.stack([np.tile(a["L0_ffn_ln1_w"], 2), np.tile(a["L0_ffn_ln2_w"], 2)], axis=1)
    d = np.arange(64)
    partner = d // HD * HD + (d % HD + HD // 2) % HD
    wq, wk, wv = (a[f"L0_ffn_{n}"] for n in ("wq", "wk", "wv"))
    got["qkv_w"] = np.concatenate([twice(wq.T), twice(wq[partner].T), twice(wk.T), twice(wk[partner[:32]].T),
                                   twice(wv.T)], axis=1)
    wo = np.zeros((NH, 32, C), f)
    wo[:, :HD] = a["L0_ffn_wo"].T.reshape(NH, HD, C)
    got["wo_w"] = wo.reshape(128, C)
    got["router_w"] = twice(a["L0_ffn_router_w"].T)
    for name, key in (("w1T", "L0_ffn_w1"), ("w3T", "L0_ffn_w3")):
        w = np.zeros((2, C, MP), f)
        w[:, :, :NE * HID] = a[key].transpose(2, 0, 1).reshape(C, NE * HID)
        got[name] = w.reshape(128, MP)
    w = np.zeros((MP, C), f)
    w[:NE * HID] = a["L0_ffn_w2"].transpose(0, 2, 1).reshape(NE * HID, C)
    got["w2T"] = w.reshape(NM, 128, C).transpose(1, 0, 2).reshape(128, -1)
    got["eye"] = np.eye(128, dtype=f)
    got["cen"] = twice(np.eye(64, dtype=f) - f(1 / 64))
    got["avg"] = twice(np.full((64, 64), 1 / 64, f))
    sel = np.zeros((128, 128), f)
    for hh in range(NH):
        sel[32 * hh + HD, 32 * hh:32 * hh + 32] = 1
    got["dsel"] = sel
    t = np.arange(T)
    got["qdec"] = np.broadcast_to((ALPHA ** t / 8).astype(f), (128, T))
    got["kdec"] = np.broadcast_to((ALPHA ** -t.astype(np.float64)).astype(f), (128, T))
    inv = (1.0 / 10000.0 ** (np.arange(0, HD, 2, dtype=f) / HD)).astype(f)
    angle = np.outer(t.astype(f), inv).astype(f)
    cos = np.tile(np.cos(angle), (1, 2)).T.astype(f)
    sin = np.concatenate([-np.sin(angle), np.sin(angle)], axis=1).T.astype(f)
    got["qcos"] = np.tile(cos, (8, 1)) * f(HD ** -0.5)
    got["qsin"] = np.tile(sin, (8, 1)) * f(HD ** -0.5)
    got["ktab"] = np.concatenate([np.tile(cos, (4, 1)), np.tile(sin, (4, 1))])
    got["rank"] = np.broadcast_to(np.arange(NE, 0, -1).astype(f), (128, NE))
    return {k: np.ascontiguousarray(v) for k, v in got.items()}


def kernel(**inputs):
    import concourse.bacc as bacc
    from concourse.bass_utils import run_bass_kernel_spmd

    nc = bacc.Bacc("TRN2", target_bir_lowering=False, num_devices=1)
    arrays = _layouts(inputs)
    args = {k: nc.dram_tensor(f"in_{k}", v.shape, mybir.dt.from_np(v.dtype), kind="ExternalInput").ap()
            for k, v in arrays.items()}
    out = nc.dram_tensor("out_layer", _OUT, mybir.dt.float32, kind="ExternalOutput").ap()
    audio_tower(nc, **args, out=out)
    r = run_bass_kernel_spmd(nc, [{f"in_{k}": v for k, v in arrays.items()}], core_ids=[0])
    return r.results[0]["out_layer"]
```
